# Optimizing a Trainium2 kernel written in Bass

```python
import numpy as np
import jax
import jax.numpy as jnp

def _softmax(x, axis=-1):
    return jax.nn.softmax(x, axis=axis)

def _gelu(x):
    return jax.nn.gelu(x, approximate=True)

def _silu(x):
    return jax.nn.silu(x)

def _sigmoid(x):
    return jax.nn.sigmoid(x)

def _layernorm(x, axis=-1, eps=1e-05):
    m = jnp.mean(x, axis=axis, keepdims=True)
    v = jnp.var(x, axis=axis, keepdims=True)
    return (x - m) / jnp.sqrt(v + eps)

def _scatter_add(tgt, idx, src, axis=0):
    return tgt.at[idx].add(src)

def _segment_sum(src, seg, n):
    return jax.ops.segment_sum(src, seg, n)
kernel_name = 'mk_dlrm_tower_d1_rec_r8_170c80'

def setup_inputs(seed: int=0):
    np.random.seed(seed)
    _w = jnp.asarray

    def _rec_inputs():
        import jax
        import jax.numpy as jnp
        _tk = jax.random.key(seed)
        ids = jnp.stack([jax.random.randint(jax.random.fold_in(_tk, 200 + f), (512,), 0, v, jnp.int32) for f, v in enumerate([1250, 12500, 125000, 12500, 1250, 1000, 12500, 1250, 12500, 125000, 1000, 1000, 1250, 12500, 12500, 12500, 12500, 1000, 1000, 1250, 1000, 125000, 1000, 1250, 1000, 1000])], axis=1)
        tbl_0 = 0.05 * jax.random.normal(jax.random.fold_in(_tk, 500 + 0), (1250, 64), jnp.float32)
        tbl_1 = 0.05 * jax.random.normal(jax.random.fold_in(_tk, 500 + 1), (12500, 64), jnp.float32)
        tbl_2 = 0.05 * jax.random.normal(jax.random.fold_in(_tk, 500 + 2), (125000, 64), jnp.float32)
        tbl_3 = 0.05 * jax.random.normal(jax.random.fold_in(_tk, 500 + 3), (12500, 64), jnp.float32)
        tbl_4 = 0.05 * jax.random.normal(jax.random.fold_in(_tk, 500 + 4), (1250, 64), jnp.float32)
        tbl_5 = 0.05 * jax.random.normal(jax.random.fold_in(_tk, 500 + 5), (1000, 64), jnp.float32)
        tbl_6 = 0.05 * jax.random.normal(jax.random.fold_in(_tk, 500 + 6), (12500, 64), jnp.float32)
        tbl_7 = 0.05 * jax.random.normal(jax.random.fold_in(_tk, 500 + 7), (1250, 64), jnp.float32)
        tbl_8 = 0.05 * jax.random.normal(jax.random.fold_in(_tk, 500 + 8), (12500, 64), jnp.float32)
        tbl_9 = 0.05 * jax.random.normal(jax.random.fold_in(_tk, 500 + 9), (125000, 64), jnp.float32)
        tbl_10 = 0.05 * jax.random.normal(jax.random.fold_in(_tk, 500 + 10), (1000, 64), jnp.float32)
        tbl_11 = 0.05 * jax.random.normal(jax.random.fold_in(_tk, 500 + 11), (1000, 64), jnp.float32)
        tbl_12 = 0.05 * jax.random.normal(jax.random.fold_in(_tk, 500 + 12), (1250, 64), jnp.float32)
        tbl_13 = 0.05 * jax.random.normal(jax.random.fold_in(_tk, 500 + 13), (12500, 64), jnp.float32)
        tbl_14 = 0.05 * jax.random.normal(jax.random.fold_in(_tk, 500 + 14), (12500, 64), jnp.float32)
        tbl_15 = 0.05 * jax.random.normal(jax.random.fold_in(_tk, 500 + 15), (12500, 64), jnp.float32)
        tbl_16 = 0.05 * jax.random.normal(jax.random.fold_in(_tk, 500 + 16), (12500, 64), jnp.float32)
        tbl_17 = 0.05 * jax.random.normal(jax.random.fold_in(_tk, 500 + 17), (1000, 64), jnp.float32)
        tbl_18 = 0.05 * jax.random.normal(jax.random.fold_in(_tk, 500 + 18), (1000, 64), jnp.float32)
        tbl_19 = 0.05 * jax.random.normal(jax.random.fold_in(_tk, 500 + 19), (1250, 64), jnp.float32)
        tbl_20 = 0.05 * jax.random.normal(jax.random.fold_in(_tk, 500 + 20), (1000, 64), jnp.float32)
        tbl_21 = 0.05 * jax.random.normal(jax.random.fold_in(_tk, 500 + 21), (125000, 64), jnp.float32)
        tbl_22 = 0.05 * jax.random.normal(jax.random.fold_in(_tk, 500 + 22), (1000, 64), jnp.float32)
        tbl_23 = 0.05 * jax.random.normal(jax.random.fold_in(_tk, 500 + 23), (1250, 64), jnp.float32)
        tbl_24 = 0.05 * jax.random.normal(jax.random.fold_in(_tk, 500 + 24), (1000, 64), jnp.float32)
        tbl_25 = 0.05 * jax.random.normal(jax.random.fold_in(_tk, 500 + 25), (1000, 64), jnp.float32)
        _rk = jax.random.fold_in(_tk, 7)
        r_dense_t = 7.22013e-05 + 1.00017 * jax.random.normal(jax.random.fold_in(_rk, 101), (512, 256), jnp.float32)
        W_top1 = 0.0360844 * jax.random.normal(jax.random.fold_in(_tk, 801), (768, 512), jnp.float32)
        W_top2 = 0.0441942 * jax.random.normal(jax.random.fold_in(_tk, 802), (512, 256), jnp.float32)
        W_top3 = 0.0625 * jax.random.normal(jax.random.fold_in(_tk, 803), (256, 1), jnp.float32)
        b_top1 = jnp.zeros((512,), jnp.float32)
        b_top2 = jnp.zeros((256,), jnp.float32)
        return (r_dense_t, ids, tbl_0, tbl_1, tbl_2, tbl_3, tbl_4, tbl_5, tbl_6, tbl_7, tbl_8, tbl_9, tbl_10, tbl_11, tbl_12, tbl_13, tbl_14, tbl_15, tbl_16, tbl_17, tbl_18, tbl_19, tbl_20, tbl_21, tbl_22, tbl_23, tbl_24, tbl_25, W_top1, b_top1, W_top2, b_top2, W_top3)
    r_dense_t, ids, tbl_0, tbl_1, tbl_2, tbl_3, tbl_4, tbl_5, tbl_6, tbl_7, tbl_8, tbl_9, tbl_10, tbl_11, tbl_12, tbl_13, tbl_14, tbl_15, tbl_16, tbl_17, tbl_18, tbl_19, tbl_20, tbl_21, tbl_22, tbl_23, tbl_24, tbl_25, W_top1, b_top1, W_top2, b_top2, W_top3 = _rec_inputs()

    def _L0_rec_setup():
        import jax, jax.numpy as jnp
        import numpy as np
        EPS = 1e-05
        NI = 33
        TRIL_I, TRIL_J = np.tril_indices(NI, k=-1)

        def layer_norm(x, g, b):
            m = jnp.mean(x, axis=-1, keepdims=True)
            v = jnp.mean(jnp.square(x - m), axis=-1, keepdims=True)
            return (x - m) * jax.lax.rsqrt(v + EPS) * g + b
        key = jax.random.key(seed)
        ks = jax.random.split(key, 8)
        B, D_DENSE, N_SP, D_SP = (4096, 256, 26, 64)
        E, PROJ, MAXD, NFLAT = (128, 32, 512, 528)
        dense_t = jax.random.normal(ks[0], (B, D_DENSE), dtype=jnp.float32)
        sparse_t = jax.random.normal(ks[1], (B, N_SP, D_SP), dtype=jnp.float32)
        Wd = jax.random.normal(ks[2], (E, D_DENSE), dtype=jnp.float32) / np.sqrt(D_DENSE)
        Ws = jax.random.normal(ks[3], (E, D_SP), dtype=jnp.float32) / np.sqrt(D_SP)
        Wsi = jax.random.normal(ks[4], (PROJ, N_SP), dtype=jnp.float32) / np.sqrt(N_SP)
        Wl = jax.random.normal(ks[5], (MAXD, NFLAT), dtype=jnp.float32) / np.sqrt(NFLAT)
        gd = jnp.ones((E,), jnp.float32)
        bd = jnp.zeros((E,), jnp.float32)
        gs = jnp.ones((E,), jnp.float32)
        bs = jnp.zeros((E,), jnp.float32)
        gsi = jnp.ones((PROJ,), jnp.float32)
        bsi = jnp.zeros((PROJ,), jnp.float32)
        gl = jnp.ones((MAXD,), jnp.float32)
        bl = jnp.zeros((MAXD,), jnp.float32)
        return {'dense_t': dense_t, 'sparse_t': sparse_t, 'Wd': Wd, 'gd': gd, 'bd': bd, 'Ws': Ws, 'gs': gs, 'bs': bs, 'Wsi': Wsi, 'gsi': gsi, 'bsi': bsi, 'Wl': Wl, 'gl': gl, 'bl': bl, 'dims_in_use': 384}
    _L0_rec_all = _L0_rec_setup()
    _L0_rec_in = {k: v for k, v in _L0_rec_all.items() if k in ('Wd', 'gd', 'bd', 'Ws', 'gs', 'bs', 'Wsi', 'gsi', 'bsi', 'Wl', 'gl', 'bl')}
    del _L0_rec_all
    return {'r_dense_t': r_dense_t, 'ids': ids, 'tbl_0': tbl_0, 'tbl_1': tbl_1, 'tbl_2': tbl_2, 'tbl_3': tbl_3, 'tbl_4': tbl_4, 'tbl_5': tbl_5, 'tbl_6': tbl_6, 'tbl_7': tbl_7, 'tbl_8': tbl_8, 'tbl_9': tbl_9, 'tbl_10': tbl_10, 'tbl_11': tbl_11, 'tbl_12': tbl_12, 'tbl_13': tbl_13, 'tbl_14': tbl_14, 'tbl_15': tbl_15, 'tbl_16': tbl_16, 'tbl_17': tbl_17, 'tbl_18': tbl_18, 'tbl_19': tbl_19, 'tbl_20': tbl_20, 'tbl_21': tbl_21, 'tbl_22': tbl_22, 'tbl_23': tbl_23, 'tbl_24': tbl_24, 'tbl_25': tbl_25, 'W_top1': W_top1, 'b_top1': b_top1, 'W_top2': W_top2, 'b_top2': b_top2, 'W_top3': W_top3, 'L0_rec_Wd': _L0_rec_in['Wd'], 'L0_rec_gd': _L0_rec_in['gd'], 'L0_rec_bd': _L0_rec_in['bd'], 'L0_rec_Ws': _L0_rec_in['Ws'], 'L0_rec_gs': _L0_rec_in['gs'], 'L0_rec_bs': _L0_rec_in['bs'], 'L0_rec_Wsi': _L0_rec_in['Wsi'], 'L0_rec_gsi': _L0_rec_in['gsi'], 'L0_rec_bsi': _L0_rec_in['bsi'], 'L0_rec_Wl': _L0_rec_in['Wl'], 'L0_rec_gl': _L0_rec_in['gl'], 'L0_rec_bl': _L0_rec_in['bl']}

def reference(r_dense_t, ids, tbl_0, tbl_1, tbl_2, tbl_3, tbl_4, tbl_5, tbl_6, tbl_7, tbl_8, tbl_9, tbl_10, tbl_11, tbl_12, tbl_13, tbl_14, tbl_15, tbl_16, tbl_17, tbl_18, tbl_19, tbl_20, tbl_21, tbl_22, tbl_23, tbl_24, tbl_25, W_top1, b_top1, W_top2, b_top2, W_top3, L0_rec_Wd, L0_rec_gd, L0_rec_bd, L0_rec_Ws, L0_rec_gs, L0_rec_bs, L0_rec_Wsi, L0_rec_gsi, L0_rec_bsi, L0_rec_Wl, L0_rec_gl, L0_rec_bl):
    import jax
    import jax.numpy as jnp

    def _L0_rec_ref(dense_t, sparse_t, Wd, gd, bd, Ws, gs, bs, Wsi, gsi, bsi, Wl, gl, bl, dims_in_use):
        import jax, jax.numpy as jnp
        import numpy as np
        EPS = 1e-05
        NI = 33
        TRIL_I, TRIL_J = np.tril_indices(NI, k=-1)

        def layer_norm(x, g, b):
            m = jnp.mean(x, axis=-1, keepdims=True)
            v = jnp.mean(jnp.square(x - m), axis=-1, keepdims=True)
            return (x - m) * jax.lax.rsqrt(v + EPS) * g + b
        x = layer_norm(dense_t @ Wd.T, gd, bd)
        y = layer_norm(jnp.einsum('bnd,ed->bne', sparse_t, Ws), gs, bs)
        y = jnp.einsum('bne,pn->bep', y, Wsi)
        y = layer_norm(y, gsi, bsi)
        y = jnp.swapaxes(y, 1, 2)
        T = jnp.concatenate([x[:, None, :], y], axis=1)
        Z = jnp.einsum('bnd,bmd->bnm', T, T)
        Zflat = Z[:, TRIL_I, TRIL_J]
        out = layer_norm(Zflat @ Wl.T, gl, bl)
        maxd = out.shape[-1]
        mask = (jnp.arange(maxd) < dims_in_use).astype(out.dtype)
        return out * mask
    e = jnp.stack([tbl_0[ids[:, 0]], tbl_1[ids[:, 1]], tbl_2[ids[:, 2]], tbl_3[ids[:, 3]], tbl_4[ids[:, 4]], tbl_5[ids[:, 5]], tbl_6[ids[:, 6]], tbl_7[ids[:, 7]], tbl_8[ids[:, 8]], tbl_9[ids[:, 9]], tbl_10[ids[:, 10]], tbl_11[ids[:, 11]], tbl_12[ids[:, 12]], tbl_13[ids[:, 13]], tbl_14[ids[:, 14]], tbl_15[ids[:, 15]], tbl_16[ids[:, 16]], tbl_17[ids[:, 17]], tbl_18[ids[:, 18]], tbl_19[ids[:, 19]], tbl_20[ids[:, 20]], tbl_21[ids[:, 21]], tbl_22[ids[:, 22]], tbl_23[ids[:, 23]], tbl_24[ids[:, 24]], tbl_25[ids[:, 25]]], axis=1)
    z = _L0_rec_ref(r_dense_t, e, L0_rec_Wd, L0_rec_gd, L0_rec_bd, L0_rec_Ws, L0_rec_gs, L0_rec_bs, L0_rec_Wsi, L0_rec_gsi, L0_rec_bsi, L0_rec_Wl, L0_rec_gl, L0_rec_bl, 384)
    z = z.reshape(z.shape[0], -1)
    h = jnp.concatenate([z, r_dense_t], axis=1)
    h = jnp.maximum(h @ W_top1 + b_top1, 0.0)
    h = jnp.maximum(h @ W_top2 + b_top2, 0.0)
    y = h @ W_top3
    return y

_drawn_inputs = setup_inputs


def setup_inputs(seed=0):
    import zlib

    import numpy as np

    out = dict(_drawn_inputs(seed))
    spreads = {'b_top1': (0.0, 0.1),
     'b_top2': (0.0, 0.1),
     'L0_rec_gd': (1.0, 0.6),
     'L0_rec_bd': (0.0, 0.8),
     'L0_rec_gs': (1.0, 0.6),
     'L0_rec_bs': (0.0, 0.1),
     'L0_rec_gsi': (1.0, 0.2),
     'L0_rec_bsi': (0.0, 0.1),
     'L0_rec_gl': (1.0, 0.2),
     'L0_rec_bl': (0.0, 0.1)}
    factors = {}
    for name, (base, spread) in spreads.items():
        noise = np.random.default_rng([zlib.crc32(name.encode()), seed]).standard_normal(out[name].shape)
        drawn = base * np.exp(spread * noise) if base else spread * noise
        out[name] = jnp.asarray(drawn.astype(out[name].dtype))
    for name, factor in factors.items():
        out[name] = (out[name] * factor).astype(out[name].dtype)
    return out
```

```python
from contextlib import ExitStack

import concourse.bass as bass
from concourse import mybir

F32 = mybir.dt.float32
I32 = mybir.dt.int32
ALU = mybir.AluOpType
ACT = mybir.ActivationFunctionType
AX = mybir.AxisListType.X

P = 128
BATCH, NSP, DSP = 512, 26, 64
E, PROJ = 128, 32
FLIN, FOUT = 512, 384
DENSE, H1, H2 = 256, 512, 256
EPS = 1e-5

GS = 4
ROWS = GS * NSP
UG = 4
US = UG * GS
UNITS = BATCH // US
BU = 8
BS = BU * US
BLOCKS = BATCH // BS
PAIRS = BATCH * NSP // P // 2
SLOTS = PAIRS // BLOCKS
JQ = PROJ // 4
KD, KZ, K1, K2 = DENSE // P, FOUT // P, H1 // P, H2 // P
FC = FLIN // P


def pairs_until(m):
    return -(-(m * 2 * ROWS) // P)


def tower(nc, table, ids, id_base, eye, gather_ones, ws_bd, ws_mask, wsi_bd, wsi_mask, rows, bs_row,
          dense, wd, wl, cols, w1, w2, out):
    with ExitStack() as ctx:
        def sb(name, shape, dt=F32):
            return ctx.enter_context(nc.sbuf_tensor(name, shape, dt))

        def ps(name):
            return ctx.enter_context(nc.psum_tensor(name, [P, 512], F32))

        def sem(name):
            return ctx.enter_context(nc.semaphore(name))

        ids_sb = sb("ids_sb", [P, 2 * PAIRS], I32)
        base_sb = sb("base_sb", [P, 2 * PAIRS], I32)
        row_id = sb("row_id", [P, 2 * PAIRS], I32)
        eye_sb = sb("eye_sb", [P, P])
        gones_sb = sb("gones_sb", [ROWS, ROWS + 1])
        ones = sb("ones", [P, P])
        ws_sb = sb("ws_sb", [P, 2 * E])
        wsm_sb = sb("wsm_sb", [P, 2 * E])
        ws_c = sb("ws_c", [P, 2 * E])
        wsi_sb = sb("wsi_sb", [ROWS, GS * PROJ])
        wsim_sb = sb("wsim_sb", [ROWS, GS * PROJ])
        wsi_0 = sb("wsi_0", [ROWS, GS * PROJ])
        wsi_c = sb("wsi_c", [ROWS + 1, GS * PROJ])
        means = sb("means", [P, 4])
        eps_c = sb("eps_c", [P, 1])
        rows_sb = sb("rows_sb", [P, 3 * E + 2 * PROJ])
        gs_b, gd_b, bd_b = (rows_sb[:, n * E:(n + 1) * E] for n in range(3))
        gsi_b = rows_sb[:, 3 * E:3 * E + PROJ]
        bsi_b = rows_sb[:, 3 * E + PROJ:3 * E + 2 * PROJ]
        dense_sb = sb("dense_sb", [P, KD, BATCH])
        wd_sb = sb("wd_sb", [P, KD, E])
        wl_sb = sb("wl_sb", [P, JQ, FLIN])
        wl_mean = sb("wl_mean", [P, 2 * JQ])
        cols_sb = sb("cols_sb", [P, K1 + 2 * K2 + 2 * KZ])
        b1_c = cols_sb[:, 0:K1]
        b2_c = cols_sb[:, K1:K1 + K2]
        w3_c = cols_sb[:, K1 + K2:K1 + 2 * K2]
        gl_c = cols_sb[:, K1 + 2 * K2:K1 + 2 * K2 + KZ]
        bl_c = cols_sb[:, K1 + 2 * K2 + KZ:K1 + 2 * K2 + 2 * KZ]
        w1_sb = sb("w1_sb", [P, KZ + KD, H1])
        w2_sb = sb("w2_sb", [P, K1, H2])

        xstat = sb("xstat", [P, 4, 6])
        xmv = sb("xmv", [P, 4, 2])
        xsd = sb("xsd", [P, 4])
        xr = sb("xr", [P, 4])
        xn = sb("xn", [P, 4, E])
        xg = sb("xg", [P, 4, E])
        xb = sb("xb", [P, 4, E])
        xT = sb("xT", [P, BATCH])

        g_sb = sb("g_sb", [P, SLOTS, P])
        sT = sb("sT", [P, SLOTS * P])
        square = sb("square", [P, 2, UG, E])
        ssA = sb("ssA", [P, 2, UG])
        sdA = sb("sdA", [P, 2, UG])
        rA = sb("rA", [P, 2, UG])
        y1 = sb("y1", [ROWS + 1, 2, UG, E])
        sqB = sb("sqB", [P, 2, US * PROJ])
        ssB = sb("ssB", [P, 2, US])
        sdB = sb("sdB", [P, 2, US])
        rB = sb("rB", [P, 2, US])
        T = sb("T", [P, 2, US, PROJ])
        Tx = sb("Tx", [P, 2, US, PROJ])
        Zt = sb("Zt", [P, BLOCKS, JQ, BS])
        sqO = sb("sqO", [P, FC * BS])
        sdO = sb("sdO", [P, BS])
        rO = sb("rO", [P, BS])
        zn = sb("zn", [P, KZ, BS])
        zT = sb("zT", [P, KZ, BATCH])
        h1T = sb("h1T", [P, K1, BATCH])
        h2T = sb("h2T", [P, K2, BATCH])
        y_sb = sb("y_sb", [1, BATCH])

        psT, psZ, psW, psS = ps("psT"), ps("psZ"), ps("psW"), ps("psS")
        psA = [ps("psA0"), ps("psA1")]
        psB = [ps("psB0"), ps("psB1")]
        psH = [psA[0], psA[1], psB[0], psB[1]]

        d_ids, d_eye, d_ws, d_wsi, d_rows = (sem(n) for n in ("d_ids", "d_eye", "d_ws", "d_wsi", "d_rows"))
        d_dense, d_wl, d_cols, d_w1, d_w2, d_out = (sem(n) for n in ("d_dense", "d_wl", "d_cols", "d_w1",
                                                                     "d_w2", "d_out"))
        gathered = [sem(f"gathered{n}") for n in range(SLOTS)]
        ids_added = sem("ids_added")
        prep = sem("prep")
        wsi_summed = sem("wsi_summed")
        x_mul, x_sd, x_tr = sem("x_mul"), sem("x_sd"), sem("x_tr")
        xT_ready = sem("xT_ready")
        wl_ready = sem("wl_ready")
        pair_transposed, sT_ready = sem("pair_transposed"), sem("sT_ready")
        A_done, A_summed, A_sd, A_recip, y1_ready = (sem(n) for n in ("A_done", "A_summed", "A_sd", "A_recip",
                                                                      "y1_ready"))
        B_done, B_squared, B_summed, B_sd, B_recip = (sem(n) for n in ("B_done", "B_squared", "B_summed", "B_sd",
                                                                       "B_recip"))
        T_normed, T_scaled, T_ready, Tx_ready = (sem(n) for n in ("T_normed", "T_scaled", "T_ready", "Tx_ready"))
        Z_done, Z_kept = sem("Z_done"), sem("Z_kept")
        W_done, W_squared, W_summed, W_sd, W_recip, W_normed, z_ready = (
            sem(n) for n in ("W_done", "W_squared", "W_summed", "W_sd", "W_recip", "W_normed", "z_ready"))
        h1_done, h1_ready, h2_done, h2_ready, y_done, y_ready = (
            sem(n) for n in ("h1_done", "h1_ready", "h2_done", "h2_ready", "y_done", "y_ready"))

        block = ctx.enter_context(nc.Block())

        @block.sync
        def _(sp):
            sp.dma_start(ids_sb[:, :], ids).then_inc(d_ids, 16)
            sp.dma_start(base_sb[:, :], id_base).then_inc(d_ids, 16)
            sp.dma_start(wd_sb[:, :, :], wd).then_inc(d_dense, 16)
            sp.dma_start(dense_sb[:, :, :], dense).then_inc(d_dense, 16)
            sp.dma_start(ws_sb[:, :], ws_bd).then_inc(d_ws, 16)
            sp.dma_start(wsm_sb[:, :], ws_mask).then_inc(d_ws, 16)
            sp.dma_start(rows_sb[:, :], rows.broadcast_to([P, rows.shape[1]])).then_inc(d_rows, 16)
            sp.dma_start(w1_sb[:, :, :], w1).then_inc(d_w1, 16)
            sp.dma_start(w2_sb[:, :, :], w2).then_inc(d_w2, 16)
            sp.wait_ge(y_ready, 1)
            sp.dma_start(out.rearrange("b o -> o b"), y_sb[:, :]).then_inc(d_out, 16)
            sp.wait_ge(d_out, 16)

        @block.gpsimd
        def _(pool):
            pool.wait_ge(d_ids, 32)
            pool.tensor_tensor(row_id[:, :], ids_sb[:, :], base_sb[:, :], ALU.add).then_inc(ids_added, 1)
            pool.wait_ge(ids_added, 1)
            for k in range(PAIRS):
                if k >= SLOTS:
                    pool.wait_ge(pair_transposed, k - SLOTS + 1)
                for h in range(2):
                    pool.indirect_dma_start(
                        g_sb[:, k % SLOTS, h * DSP:(h + 1) * DSP], None, table,
                        bass.IndirectOffsetOnAxis(row_id[:, 2 * k + h:2 * k + h + 1], 0),
                    ).then_inc(gathered[k % SLOTS], 16)

        @block.tensor
        def _(pe):
            def transposes(u, m):
                if m or u:
                    pe.wait_ge(sT_ready, u)
                for n, k in enumerate(range(pairs_until(m), pairs_until(m + 1))):
                    pe.wait_ge(gathered[k], 32 * (u // BU + 1))
                    pe.transpose(psT[:, n * P:(n + 1) * P], g_sb[:, k, :], eye_sb[:, :]).then_inc(pair_transposed, 1)

            def project(u, m):
                pe.wait_ge(sT_ready, u + 1)
                if u >= 2:
                    pe.wait_ge(y1_ready, u - 1)
                for g in range(2):
                    mm = pe.matmul(psA[m % 2][0:ROWS, g * 2 * E:(g + 1) * 2 * E],
                                   sT[:, (2 * m + g) * ROWS:(2 * m + g + 1) * ROWS], ws_c[:, :],
                                   start=True, stop=True)
                mm.then_inc(A_done, 1)

            def mix(u, m):
                pe.wait_ge(y1_ready, u + 1)
                if u >= 2:
                    pe.wait_ge(T_normed, u - 1)
                for g in range(UG):
                    mm = pe.matmul(psB[m % 2][:, g * P:(g + 1) * P], y1[:, m % 2, g, :], wsi_c[:, :],
                                   start=True, stop=True)
                mm.then_inc(B_done, 1)

            def inner(u, m):
                pe.wait_ge(Tx_ready, u + 1)
                if u >= 1:
                    pe.wait_ge(Z_kept, u)
                for g in range(UG):
                    mm = pe.matmul(psZ[:, g * P:(g + 1) * P],
                                   T[:, m % 2, g * GS:(g + 1) * GS, :].rearrange("p c i -> p (c i)"),
                                   Tx[:, m % 2, g * GS:(g + 1) * GS, :].rearrange("p c j -> p (c j)"),
                                   start=True, stop=True)
                mm.then_inc(Z_done, 1)

            def linear(b, lo, hi):
                if lo == 0:
                    pe.wait_ge(Z_kept, BU * (b + 1))
                    if b >= 1:
                        pe.wait_ge(W_normed, b)
                    else:
                        pe.wait_ge(wl_ready, 1)
                for n in range(lo, hi):
                    f, j = n // JQ, n % JQ
                    mm = pe.matmul(psW[:, f * BS:(f + 1) * BS], wl_sb[:, j, f * P:(f + 1) * P], Zt[:, b, j, :],
                                   start=(j == 0), stop=(j == JQ - 1))
                if hi == FC * JQ:
                    mm.then_inc(W_done, 1)

            def linear_sums(b):
                pe.wait_ge(W_squared, b + 1)
                if b >= 1:
                    pe.wait_ge(W_sd, b)
                for f in range(FC):
                    mm = pe.matmul(psS[:, 0:BS], ones[:, :], sqO[:, f * BS:(f + 1) * BS],
                                   start=(f == 0), stop=(f == FC - 1))
                mm.then_inc(W_summed, 1)

            pe.wait_ge(d_dense, 32)
            for s in range(4):
                for k in range(KD):
                    mm = pe.matmul(psB[0][:, s * E:(s + 1) * E], dense_sb[:, k, s * P:(s + 1) * P],
                                   wd_sb[:, k, :], start=(k == 0), stop=(k == KD - 1))
            mm.then_inc(x_mul, 1)
            pe.wait_ge(d_eye, 32)
            pe.wait_ge(prep, 6)
            pe.matmul(psW[0:ROWS + 1, 0:GS * PROJ], gones_sb[:, :], wsi_0[:, :], start=True,
                      stop=True).then_inc(wsi_summed, 1)

            def step(t):
                b, n = (t - 10) // BU, (t - 10) % BU
                if 0 <= b < BLOCKS - 1 and n < 6:
                    cut = [0, 6, 12, 17, 22, 27, 32]
                    linear(b, cut[n], cut[n + 1])
                if 0 <= t - 2 < UNITS:
                    inner(t - 2, (t - 2) % BU)
                if 0 <= t < UNITS:
                    mix(t, t % BU)
                if 0 <= b < BLOCKS - 1 and n == 6:
                    linear_sums(b)
                if t == 0:
                    pe.wait_ge(x_tr, 1)
                    for s in range(4):
                        mm = pe.transpose(psS[:, s * P:(s + 1) * P], xb[:, s, :], eye_sb[:, :])
                    mm.then_inc(x_tr, 1)
                if 0 <= t + 2 < UNITS:
                    project(t + 2, (t + 2) % BU)
                if 0 <= t + 3 < UNITS:
                    transposes(t + 3, (t + 3) % BU)

            for t in range(-3, UNITS + 1):
                if t == -2:
                    pe.wait_ge(prep, 8)
                step(t)

            pe.wait_ge(T_normed, UNITS)
            pe.wait_ge(y1_ready, UNITS)
            pe.wait_ge(d_w1, 16)
            for f in range(K1):
                for k in range(KD):
                    pe.matmul(psH[f][:, :], w1_sb[:, KZ + k, f * P:(f + 1) * P], dense_sb[:, k, :],
                              start=(k == 0), stop=False)
            inner(UNITS - 1, BU - 1)
            for f in range(K1):
                for k in range(KZ):
                    pe.wait_ge(z_ready, BLOCKS - 1)
                    pe.matmul(psH[f][:, 0:BATCH - BS], w1_sb[:, k, f * P:(f + 1) * P], zT[:, k, 0:BATCH - BS],
                              start=False, stop=False)
            linear(BLOCKS - 1, 0, FC * JQ)
            linear_sums(BLOCKS - 1)
            pe.wait_ge(z_ready, BLOCKS)
            for f in range(K1):
                for k in range(KZ):
                    mm = pe.matmul(psH[f][:, BATCH - BS:BATCH], w1_sb[:, k, f * P:(f + 1) * P],
                                   zT[:, k, BATCH - BS:BATCH], start=False, stop=(k == KZ - 1))
                mm.then_inc(h1_done, 1)
            pe.wait_ge(d_w2, 16)
            for k in range(K1):
                pe.wait_ge(h1_ready, k + 1)
                for f in range(K2):
                    mm = pe.matmul((psZ, psW)[f][:, :], w2_sb[:, k, f * P:(f + 1) * P], h1T[:, k, :],
                                   start=(k == 0), stop=(k == K1 - 1))
                    if k == K1 - 1:
                        mm.then_inc(h2_done, 1)
            for k in range(K2):
                pe.wait_ge(h2_ready, k + 1)
                mm = pe.matmul(psS[0:1, :], w3_c[:, k:k + 1], h2T[:, k, :], start=(k == 0), stop=(k == K2 - 1))
            mm.then_inc(y_done, 1)

        @block.scalar
        def _(act):
            def rows_out(u, m):
                lo, hi = pairs_until(m), pairs_until(m + 1)
                act.wait_ge(pair_transposed, SLOTS * (u // BU) + hi)
                if u >= BU:
                    act.wait_ge(A_done, u - BU + 2)
                act.activation(sT[:, lo * P:hi * P], psT[:, 0:(hi - lo) * P], ACT.Copy).then_inc(sT_ready, 1)

            def squares_a(u, m):
                act.wait_ge(A_done, u + 1)
                for g in range(UG):
                    last = act.activation(square[0:ROWS, m % 2, g, :], psA[m % 2][0:ROWS, g * E:(g + 1) * E], ACT.Square,
                                          accum_out=ssA[0:ROWS, m % 2, g:g + 1])
                last.then_inc(A_summed, 1)

            def deviation_a(u, m):
                act.wait_ge(A_summed, u + 1)
                if u >= 2:
                    act.wait_ge(A_recip, u - 1)
                act.activation(sdA[0:ROWS, m % 2, :], ssA[0:ROWS, m % 2, :], ACT.Sqrt, bias=eps_c[0:ROWS, :],
                               scale=1.0 / E).then_inc(A_sd, 1)

            def squares_b(u, m):
                act.wait_ge(B_done, u + 1)
                if u >= 2:
                    act.wait_ge(B_summed, u - 1)
                act.activation(sqB[:, m % 2, :], psB[m % 2][:, :], ACT.Square).then_inc(B_squared, 1)

            def deviation_b(u, m):
                act.wait_ge(B_summed, u + 1)
                if u >= 2:
                    act.wait_ge(B_recip, u - 1)
                act.activation(sdB[:, m % 2, :], ssB[:, m % 2, :], ACT.Sqrt, bias=eps_c[:, :],
                               scale=1.0 / PROJ).then_inc(B_sd, 1)

            def with_x(u, m):
                if u >= 2:
                    act.wait_ge(Z_done, u - 1)
                else:
                    act.wait_ge(xT_ready, 1)
                act.activation(Tx[:, m % 2, :, 0:1], xT[:, u * US:(u + 1) * US].rearrange("p (s o) -> p s o", o=1),
                               ACT.Copy)
                act.wait_ge(T_ready, u + 1)
                act.activation(Tx[:, m % 2, :, 1:PROJ], T[:, m % 2, :, 0:PROJ - 1], ACT.Copy).then_inc(Tx_ready, 1)

            def keep_z(u, m):
                act.wait_ge(Z_done, u + 1)
                b = u // BU
                for c in range(GS):
                    src = psZ[c * PROJ:(c + 1) * PROJ, :].rearrange("p (g q j) -> p g q j", g=UG, j=JQ)
                    for q in range(4):
                        dst = Zt[q * PROJ:(q + 1) * PROJ, b, :, m * US:(m + 1) * US].rearrange(
                            "p j (g c) -> p g c j", c=GS)
                        last = act.activation(dst[:, :, c, :], src[:, :, 4 * c + q, :], ACT.Copy)
                last.then_inc(Z_kept, 1)

            def squares_w(b):
                act.wait_ge(W_done, b + 1)
                if b >= 1:
                    act.wait_ge(W_summed, b)
                act.activation(sqO[:, :], psW[:, :], ACT.Square).then_inc(W_squared, 1)

            def deviation_w(b):
                act.wait_ge(W_summed, b + 1)
                if b >= 1:
                    act.wait_ge(W_recip, b)
                act.activation(sdO[:, :], psS[:, 0:BS], ACT.Sqrt, bias=eps_c[:, :],
                               scale=1.0 / FLIN).then_inc(W_sd, 1)

            def scale_z(b):
                act.wait_ge(W_normed, b + 1)
                for k in range(KZ):
                    last = act.activation(zT[:, k, b * BS:(b + 1) * BS], zn[:, k, :], ACT.Identity,
                                          bias=bl_c[:, k:k + 1], scale=gl_c[:, k:k + 1])
                last.then_inc(z_ready, 1)

            act.dma_start(wsi_sb[:, :], wsi_bd).then_inc(d_wsi, 16)
            act.dma_start(wsim_sb[:, :], wsi_mask).then_inc(d_wsi, 16)
            act.dma_start(eye_sb[:, :], eye).then_inc(d_eye, 16)
            act.dma_start(gones_sb[:, :], gather_ones).then_inc(d_eye, 16)
            for n in range(2):
                for g in range(UG):
                    act.dma_start(y1[ROWS:ROWS + 1, n, g, :], bs_row).then_inc(d_rows, 16)
            act.dma_start(wl_sb[:, :, :], wl).then_inc(d_wl, 16)
            act.dma_start(cols_sb[:, :], cols).then_inc(d_cols, 16)
            act.wait_ge(prep, 10)
            act.activation(xsd[:, :], xmv[:, :, 1], ACT.Sqrt, bias=eps_c[:, :]).then_inc(x_sd, 1)

            def step(t):
                if t == 2:
                    act.wait_ge(x_tr, 2)
                    act.activation(xT[:, :], psS[:, :], ACT.Copy).then_inc(xT_ready, 1)
                if 0 <= t - 2 < UNITS:
                    with_x(t - 2, (t - 2) % BU)
                if 0 <= t + 2 < UNITS:
                    rows_out(t + 2, (t + 2) % BU)
                if 0 <= t + 1 < UNITS:
                    squares_a(t + 1, (t + 1) % BU)
                if 0 <= t - 1 < UNITS:
                    deviation_b(t - 1, (t - 1) % BU)
                if 0 <= t + 1 < UNITS:
                    deviation_a(t + 1, (t + 1) % BU)
                b, n = (t - 10) // BU, (t - 10) % BU
                if 0 <= b < BLOCKS - 1 and n == 7:
                    deviation_w(b)
                if 0 <= t - 2 < UNITS:
                    keep_z(t - 2, (t - 2) % BU)
                if 0 <= t < UNITS:
                    squares_b(t, t % BU)
                if 0 <= b < BLOCKS - 1 and n == 6:
                    squares_w(b)
                if 0 <= b < BLOCKS - 1 and n == 7:
                    scale_z(b)

            for t in range(-2, UNITS + 2):
                if t == 10:
                    act.wait_ge(d_cols, 16)
                step(t)
            squares_w(BLOCKS - 1)
            deviation_w(BLOCKS - 1)
            scale_z(BLOCKS - 1)
            for f in range(K1):
                act.wait_ge(h1_done, f + 1)
                act.activation(h1T[:, f, :], psH[f][:, :], ACT.Relu, bias=b1_c[:, f:f + 1]).then_inc(h1_ready, 1)
            for f in range(K2):
                act.wait_ge(h2_done, f + 1)
                act.activation(h2T[:, f, :], (psZ, psW)[f][:, :], ACT.Relu,
                               bias=b2_c[:, f:f + 1]).then_inc(h2_ready, 1)

        @block.vector
        def _(dve):
            def recip_a(u, m):
                dve.wait_ge(A_sd, u + 1)
                dve.reciprocal(rA[0:ROWS, m % 2, :], sdA[0:ROWS, m % 2, :]).then_inc(A_recip, 1)

            def norm_a(u, m):
                dve.wait_ge(A_recip, u + 1)
                if u >= 2:
                    dve.wait_ge(B_done, u - 1)
                for g in range(UG):
                    last = dve.scalar_tensor_tensor(
                        out=y1[0:ROWS, m % 2, g, :], in0=psA[m % 2][0:ROWS, g * E:(g + 1) * E],
                        scalar=rA[0:ROWS, m % 2, g:g + 1], in1=gs_b[0:ROWS, :], op0=ALU.mult, op1=ALU.mult)
                last.then_inc(y1_ready, 1)

            def sums_b(u, m):
                dve.wait_ge(B_squared, u + 1)
                dve.tensor_reduce(ssB[:, m % 2, :], sqB[:, m % 2, :].rearrange("p (s j) -> p s j", j=PROJ),
                                  AX, ALU.add).then_inc(B_summed, 1)

            def recip_b(u, m):
                dve.wait_ge(B_sd, u + 1)
                dve.reciprocal(rB[:, m % 2, :], sdB[:, m % 2, :]).then_inc(B_recip, 1)

            def norm_b(u, m):
                t = T[:, m % 2, :, :]
                dve.wait_ge(B_recip, u + 1)
                if u >= 2:
                    dve.wait_ge(Z_done, u - 1)
                dve.tensor_tensor(t, psB[m % 2][:, :].rearrange("p (s j) -> p s j", j=PROJ),
                                  rB[:, m % 2, :].rearrange("p (s o) -> p s o", o=1).broadcast_to([P, US, PROJ]),
                                  ALU.mult).then_inc(T_normed, 1)
                dve.wait_ge(T_normed, u + 1)
                dve.tensor_tensor(t, t, gsi_b.rearrange("p (o j) -> p o j", o=1).broadcast_to([P, US, PROJ]),
                                  ALU.mult).then_inc(T_scaled, 1)
                dve.wait_ge(T_scaled, u + 1)
                dve.tensor_tensor(t, t, bsi_b.rearrange("p (o j) -> p o j", o=1).broadcast_to([P, US, PROJ]),
                                  ALU.add).then_inc(T_ready, 1)

            def recip_w(b):
                dve.wait_ge(W_sd, b + 1)
                dve.reciprocal(rO[:, :], sdO[:, :]).then_inc(W_recip, 1)

            def norm_w(b):
                dve.wait_ge(W_recip, b + 1)
                if b >= 1:
                    dve.wait_ge(z_ready, b)
                dve.tensor_tensor(zn[:, :, :], psW[:, 0:KZ * BS].rearrange("p (k s) -> p k s", k=KZ),
                                  rO[:, :].rearrange("p (o s) -> p o s", o=1).broadcast_to([P, KZ, BS]),
                                  ALU.mult).then_inc(W_normed, 1)

            dve.memset(eps_c[:, :], EPS).then_inc(prep, 1)
            dve.memset(ones[:, :], 1.0).then_inc(prep, 1)
            dve.wait_ge(d_wsi, 32)
            dve.tensor_reduce(means[0:ROWS, 0:1], wsi_sb[:, :], AX, ALU.add).then_inc(prep, 1)
            dve.wait_ge(d_ws, 32)
            dve.tensor_reduce(means[:, 1:2], ws_sb[:, :], AX, ALU.add).then_inc(prep, 1)
            dve.wait_ge(prep, 4)
            dve.tensor_scalar(means[0:ROWS, 2:3], means[0:ROWS, 0:1], -1.0 / PROJ, None, ALU.mult)
            dve.tensor_scalar(means[:, 3:4], means[:, 1:2], -1.0 / E, None, ALU.mult).then_inc(prep, 1)
            dve.wait_ge(prep, 5)
            dve.scalar_tensor_tensor(out=wsi_0[:, :], in0=wsim_sb[:, :], scalar=means[0:ROWS, 2:3],
                                     in1=wsi_sb[:, :], op0=ALU.mult, op1=ALU.add).then_inc(prep, 1)
            dve.scalar_tensor_tensor(out=ws_c[:, :], in0=wsm_sb[:, :], scalar=means[:, 3:4],
                                     in1=ws_sb[:, :], op0=ALU.mult, op1=ALU.add).then_inc(prep, 1)
            dve.wait_ge(wsi_summed, 1)
            dve.tensor_copy(wsi_c[:, :], psW[0:ROWS + 1, 0:GS * PROJ]).then_inc(prep, 1)
            dve.wait_ge(x_mul, 1)
            for s in range(4):
                last = dve.bn_stats(xstat[:, s, :], psB[0][:, s * E:(s + 1) * E])
            last.then_inc(prep, 1)
            dve.wait_ge(prep, 9)
            for s in range(4):
                last = dve.bn_aggr(xmv[:, s, :], xstat[:, s, :])
            last.then_inc(prep, 1)
            dve.wait_ge(x_sd, 1)
            dve.reciprocal(xr[:, :], xsd[:, :]).then_inc(prep, 1)
            dve.wait_ge(prep, 11)
            for s in range(4):
                last = dve.tensor_scalar(xn[:, s, :], psB[0][:, s * E:(s + 1) * E], xmv[:, s, 0:1], xr[:, s:s + 1],
                                         ALU.subtract, ALU.mult)
            last.then_inc(prep, 1)
            dve.wait_ge(prep, 12)
            dve.wait_ge(d_rows, 16 * (1 + 2 * UG))
            dve.tensor_tensor(xg[:, :, :], xn[:, :, :],
                              gd_b.rearrange("p (o e) -> p o e", o=1).broadcast_to([P, 4, E]),
                              ALU.mult).then_inc(prep, 1)
            dve.wait_ge(prep, 13)
            dve.tensor_tensor(xb[:, :, :], xg[:, :, :],
                              bd_b.rearrange("p (o e) -> p o e", o=1).broadcast_to([P, 4, E]),
                              ALU.add).then_inc(x_tr, 1)

            def center_wl(j):
                if j == 0:
                    dve.wait_ge(d_wl, 16)
                    dve.tensor_reduce(wl_mean[:, 0:JQ], wl_sb[:, :, :], AX, ALU.add).then_inc(prep, 1)
                    dve.wait_ge(prep, 14)
                    dve.tensor_scalar(wl_mean[:, JQ:2 * JQ], wl_mean[:, 0:JQ], 1.0 / FLIN, None,
                                      ALU.mult).then_inc(prep, 1)
                    dve.wait_ge(prep, 15)
                last = dve.tensor_scalar(wl_sb[:, j, :], wl_sb[:, j, :], wl_mean[:, JQ + j:JQ + j + 1], None,
                                         ALU.subtract)
                if j == JQ - 1:
                    last.then_inc(wl_ready, 1)

            def step(t):
                if 0 <= t - 1 < UNITS:
                    sums_b(t - 1, (t - 1) % BU)
                if 0 <= t < UNITS:
                    recip_a(t, t % BU)
                    norm_a(t, t % BU)
                if 0 <= t - 1 < UNITS:
                    recip_b(t - 1, (t - 1) % BU)
                    norm_b(t - 1, (t - 1) % BU)
                if t == 0:
                    for j in range(JQ):
                        center_wl(j)
                b, n = (t - 10) // BU, (t - 10) % BU
                if 0 <= b < BLOCKS - 1 and n == 7:
                    recip_w(b)
                    norm_w(b)

            for t in range(0, UNITS + 2):
                step(t)
            recip_w(BLOCKS - 1)
            norm_w(BLOCKS - 1)
            dve.wait_ge(y_done, 1)
            dve.tensor_copy(y_sb[:, :], psS[0:1, :]).then_inc(y_ready, 1)


def kernel(**inputs):
    import numpy as np
    import concourse.bacc as bacc
    from concourse.bass_utils import run_bass_kernel_spmd

    x = {k: np.asarray(v) for k, v in inputs.items()}
    tables = [x[f"tbl_{n}"] for n in range(NSP)]

    def chunks(a):
        return np.ascontiguousarray(a.reshape(-1, 2, ROWS).transpose(1, 0, 2).reshape(2, PAIRS, P)
                                    .transpose(2, 1, 0).reshape(P, 2 * PAIRS))

    def on_partitions(a):
        return np.ascontiguousarray(a.reshape(-1, P, a.shape[1]).transpose(1, 0, 2))

    def diagonal(a, n):
        d = np.zeros((n, a.shape[0], n, a.shape[1]), a.dtype)
        for i in range(n):
            d[i, :, i, :] = a
        return d.reshape(n * a.shape[0], n * a.shape[1])

    starts = np.cumsum([0] + [t.shape[0] for t in tables[:-1]]).astype(np.int32)
    gather_ones = np.eye(ROWS, ROWS + 1, dtype=np.float32)
    gather_ones[:, ROWS] = 1.0
    q, i, j = np.meshgrid(np.arange(4), np.arange(1, PROJ + 1), np.arange(JQ), indexing="ij")
    j = q * JQ + j
    pairs = PROJ * (PROJ + 1) // 2
    at = np.where(i > j, i * (i - 1) // 2 + j, pairs).reshape(P, JQ)
    wl = x["L0_rec_Wl"].T
    wl = np.concatenate([wl, np.zeros((1, FLIN), wl.dtype)])[at]
    w1 = x["W_top1"]
    arrays = {
        "table": np.concatenate(tables, axis=0),
        "ids": chunks(x["ids"]),
        "id_base": chunks(np.broadcast_to(starts, (BATCH, NSP))),
        "eye": np.eye(P, dtype=np.float32),
        "gather_ones": gather_ones,
        "ws_bd": diagonal(x["L0_rec_Ws"].T, 2),
        "ws_mask": diagonal(np.ones((DSP, E), np.float32), 2),
        "wsi_bd": diagonal(x["L0_rec_Wsi"].T, GS),
        "wsi_mask": diagonal(np.ones((NSP, PROJ), np.float32), GS),
        "rows": np.concatenate([x[f"L0_rec_{n}"] for n in ("gs", "gd", "bd", "gsi", "bsi")])[None, :],
        "bs_row": x["L0_rec_bs"][None, :],
        "dense": on_partitions(x["r_dense_t"].T),
        "wd": on_partitions(x["L0_rec_Wd"].T),
        "wl": wl,
        "cols": np.ascontiguousarray(np.concatenate([
            x["b_top1"].reshape(K1, P), x["b_top2"].reshape(K2, P), x["W_top3"].reshape(K2, P),
            x["L0_rec_gl"][:FOUT].reshape(KZ, P), x["L0_rec_bl"][:FOUT].reshape(KZ, P)]).T),
        "w1": on_partitions(np.concatenate([w1[:FOUT], w1[FLIN:]])),
        "w2": on_partitions(x["W_top2"]),
    }
    nc = bacc.Bacc("TRN2", target_bir_lowering=False, num_devices=1)
    args = [nc.dram_tensor(f"in_{n}", a.shape, mybir.dt.from_np(a.dtype), kind="ExternalInput").ap()
            for n, a in arrays.items()]
    out = nc.dram_tensor("out_y", (BATCH, 1), F32, kind="ExternalOutput").ap()
    tower(nc, *args, out)
    r = run_bass_kernel_spmd(nc, [{f"in_{n}": a for n, a in arrays.items()}], core_ids=[0])
    return r.results[0]["out_y"]
```

```python
from contextlib import ExitStack

import concourse.bass as bass
from concourse import mybir

F32 = mybir.dt.float32
I32 = mybir.dt.int32
ALU = mybir.AluOpType
ACT = mybir.ActivationFunctionType
AX = mybir.AxisListType.X

P = 128
BATCH, NSP, DSP = 512, 26, 64
E, PROJ = 128, 32
FLIN, FOUT = 512, 384
DENSE, H1, H2 = 256, 512, 256
EPS = 1e-5

GS = 4
ROWS = GS * NSP
UG = 4
US = UG * GS
UNITS = BATCH // US
BU = 8
BS = BU * US
BLOCKS = BATCH // BS
PAIRS = BATCH * NSP // P // 2
SLOTS = PAIRS // BLOCKS
JQ = PROJ // 4
KD, KZ, K1, K2 = DENSE // P, FOUT // P, H1 // P, H2 // P
FC = FLIN // P
SMALL = [0]
for width in (KD * E, 2 * E, 2 * E, GS * PROJ, GS * PROJ, ROWS + 1, P, K1 + 2 * K2 + 2 * KZ):
    SMALL.append(SMALL[-1] + width)


def pairs_until(m):
    return -(-(m * 2 * ROWS) // P)


def tower(nc, table, ids, small, rows, bs_rows, dense, wl, w1, w2, out):
    with ExitStack() as ctx:
        def sb(name, shape, dt=F32):
            return ctx.enter_context(nc.sbuf_tensor(name, shape, dt))

        def ps(name):
            return ctx.enter_context(nc.psum_tensor(name, [P, 512], F32))

        def sem(name):
            return ctx.enter_context(nc.semaphore(name))

        ids_sb = sb("ids_sb", [P, 2, 2 * PAIRS], I32)
        row_id = sb("row_id", [P, 2 * PAIRS], I32)
        small_sb = sb("small_sb", [P, SMALL[-1]])
        (wd_f, ws_sb, wsm_sb, wsi_sb, wsim_sb, gones_sb, eye_sb, cols_sb) = (
            small_sb[:, lo:hi] for lo, hi in zip(SMALL[:-1], SMALL[1:]))
        wd_sb = wd_f.rearrange("p (k e) -> p k e", k=KD)
        b1_c = cols_sb[:, 0:K1]
        b2_c = cols_sb[:, K1:K1 + K2]
        w3_c = cols_sb[:, K1 + K2:K1 + 2 * K2]
        gl_c = cols_sb[:, K1 + 2 * K2:K1 + 2 * K2 + KZ]
        bl_c = cols_sb[:, K1 + 2 * K2 + KZ:K1 + 2 * K2 + 2 * KZ]
        rows_sb = sb("rows_sb", [P, 3 * E + 2 * PROJ])
        gs_b, gd_b, bd_b = (rows_sb[:, n * E:(n + 1) * E] for n in range(3))
        gsi_b = rows_sb[:, 3 * E:3 * E + PROJ]
        bsi_b = rows_sb[:, 3 * E + PROJ:3 * E + 2 * PROJ]
        ones = sb("ones", [P, P])
        eps_c = sb("eps_c", [P, 1])
        means = sb("means", [P, 4])
        ws_c = sb("ws_c", [P, 2 * E])
        wsi_0 = sb("wsi_0", [ROWS, GS * PROJ])
        wsi_c = sb("wsi_c", [ROWS + 1, GS * PROJ])
        dense_sb = sb("dense_sb", [P, KD, BATCH])
        wl_sb = sb("wl_sb", [P, JQ, FLIN])
        wl_mean = sb("wl_mean", [P, 2 * JQ])
        w1_sb = sb("w1_sb", [P, KZ + KD, H1])
        w2_sb = sb("w2_sb", [P, K1, H2])

        xstat = sb("xstat", [P, 4, 6])
        xmv = sb("xmv", [P, 4, 2])
        xsd = sb("xsd", [P, 4])
        xr = sb("xr", [P, 4])
        xn = sb("xn", [P, 4, E])
        xg = sb("xg", [P, 4, E])
        xb = sb("xb", [P, 4, E])
        xT = sb("xT", [P, BATCH])

        g_sb = sb("g_sb", [P, SLOTS, P])
        sT = sb("sT", [P, SLOTS * P])
        square = sb("square", [P, 2, UG, E])
        ssA = sb("ssA", [P, 2, UG])
        sdA = sb("sdA", [P, 2, UG])
        rA = sb("rA", [P, 2, UG])
        y1 = sb("y1", [ROWS + 1, 2, UG, E])
        sqB = sb("sqB", [P, 2, US * PROJ])
        ssB = sb("ssB", [P, 2, US])
        sdB = sb("sdB", [P, 2, US])
        rB = sb("rB", [P, 2, US])
        T = sb("T", [P, 2, US, PROJ])
        Tx = sb("Tx", [P, 2, US, PROJ])
        Zt = sb("Zt", [P, BLOCKS, JQ, BS])
        sqO = sb("sqO", [P, FC * BS])
        sdO = sb("sdO", [P, BS])
        rO = sb("rO", [P, BS])
        zn = sb("zn", [P, KZ, BS])
        zT = sb("zT", [P, KZ, BATCH])
        hd = sb("hd", [P, K1, BATCH])
        h1s = sb("h1s", [P, K1, BATCH])
        h1T = sb("h1T", [P, K1, BATCH])
        h2T = sb("h2T", [P, K2, BATCH])
        y_sb = sb("y_sb", [1, BATCH])

        psT, psZ = ps("psT"), ps("psZ")
        psS = psT[:, 2 * P:2 * P + BS]
        psW = [ps("psW0"), ps("psW1")]
        psA = [ps("psA0"), ps("psA1")]
        psB = [ps("psB0"), ps("psB1")]
        psH = [psA[0], psA[1], psB[0], psB[1]]

        d_ids, d_small, d_rows, d_bs, d_dense, d_wl, d_w1, d_w2, d_out = (
            sem(n) for n in ("d_ids", "d_small", "d_rows", "d_bs", "d_dense", "d_wl", "d_w1", "d_w2", "d_out"))
        gathered = [sem(f"gathered{n}") for n in range(SLOTS)]
        ids_added = sem("ids_added")
        prep = sem("prep")
        wsi_summed = sem("wsi_summed")
        x_mul, x_sd, x_tr = sem("x_mul"), sem("x_sd"), sem("x_tr")
        xT_ready = sem("xT_ready")
        wl_ready = sem("wl_ready")
        pair_transposed, sT_ready = sem("pair_transposed"), sem("sT_ready")
        A_done, A_summed, A_sd, A_recip, y1_ready = (sem(n) for n in ("A_done", "A_summed", "A_sd", "A_recip",
                                                                      "y1_ready"))
        B_done, B_squared, B_summed, B_sd, B_recip = (sem(n) for n in ("B_done", "B_squared", "B_summed", "B_sd",
                                                                       "B_recip"))
        T_normed, T_scaled, T_ready, Tx_ready = (sem(n) for n in ("T_normed", "T_scaled", "T_ready", "Tx_ready"))
        Z_done, Z_kept = sem("Z_done"), sem("Z_kept")
        W_done, W_squared, W_summed, W_sd, W_recip, W_normed, z_ready = (
            sem(n) for n in ("W_done", "W_squared", "W_summed", "W_sd", "W_recip", "W_normed", "z_ready"))
        h1_done, h1_ready, h2_done, h2_ready, y_done, y_ready = (
            sem(n) for n in ("h1_done", "h1_ready", "h2_done", "h2_ready", "y_done", "y_ready"))
        hd_done, hd_ready, h1_sum = sem("hd_done"), sem("hd_ready"), sem("h1_sum")
        WSI_0, WS_C, WSI_C, X_MV = 6, 7, 8, 10

        block = ctx.enter_context(nc.Block())

        @block.sync
        def _(sp):
            sp.dma_start(ids_sb[:, :, :], ids).then_inc(d_ids, 16)
            sp.dma_start(small_sb[:, :], small).then_inc(d_small, 16)
            sp.dma_start(wl_sb[:, :, :], wl).then_inc(d_wl, 16)
            sp.dma_start(w2_sb[:, :, :], w2).then_inc(d_w2, 16)
            sp.wait_ge(y_ready, 1)
            sp.dma_start(out.rearrange("b o -> o b"), y_sb[:, :]).then_inc(d_out, 16)
            sp.wait_ge(d_out, 16)

        @block.gpsimd
        def _(pool):
            pool.wait_ge(d_ids, 16)
            pool.tensor_tensor(row_id[:, :], ids_sb[:, 0, :], ids_sb[:, 1, :], ALU.add).then_inc(ids_added, 1)
            pool.wait_ge(ids_added, 1)
            for k in range(PAIRS):
                if k >= SLOTS:
                    pool.wait_ge(pair_transposed, k - SLOTS + 1)
                for h in range(2):
                    pool.indirect_dma_start(
                        g_sb[:, k % SLOTS, h * DSP:(h + 1) * DSP], None, table,
                        bass.IndirectOffsetOnAxis(row_id[:, 2 * k + h:2 * k + h + 1], 0),
                    ).then_inc(gathered[k % SLOTS], 16)

        @block.tensor
        def _(pe):
            def transposes(u, m):
                if u:
                    pe.wait_ge(sT_ready, u)
                if u >= 2 * BU + 6 and m == 6:
                    pe.wait_ge(W_sd, u // BU - 1)
                for n, k in enumerate(range(pairs_until(m), pairs_until(m + 1))):
                    pe.wait_ge(gathered[k], 32 * (u // BU + 1))
                    pe.transpose(psT[:, n * P:(n + 1) * P], g_sb[:, k, :], eye_sb).then_inc(pair_transposed, 1)

            def project(u, m):
                pe.wait_ge(sT_ready, u + 1)
                if u >= 2:
                    pe.wait_ge(y1_ready, u - 1)
                for g in range(2):
                    mm = pe.matmul(psA[m % 2][0:ROWS, g * 2 * E:(g + 1) * 2 * E],
                                   sT[:, (2 * m + g) * ROWS:(2 * m + g + 1) * ROWS], ws_c[:, :],
                                   start=True, stop=True)
                mm.then_inc(A_done, 1)

            def mix(u, m):
                pe.wait_ge(y1_ready, u + 1)
                if u == 0:
                    pe.wait_ge(prep, WSI_C)
                    pe.wait_ge(d_bs, 16)
                if u >= 2:
                    pe.wait_ge(T_normed, u - 1)
                for g in range(UG):
                    mm = pe.matmul(psB[m % 2][:, g * P:(g + 1) * P], y1[:, m % 2, g, :], wsi_c[:, :],
                                   start=True, stop=True)
                mm.then_inc(B_done, 1)

            def inner(u, m):
                pe.wait_ge(Tx_ready, u + 1)
                if u >= 1:
                    pe.wait_ge(Z_kept, u)
                for g in range(UG):
                    mm = pe.matmul(psZ[:, g * P:(g + 1) * P],
                                   T[:, m % 2, g * GS:(g + 1) * GS, :].rearrange("p c i -> p (c i)"),
                                   Tx[:, m % 2, g * GS:(g + 1) * GS, :].rearrange("p c j -> p (c j)"),
                                   start=True, stop=True)
                mm.then_inc(Z_done, 1)

            def linear(b, lo, hi, s0=0, s1=BS):
                if lo == 0:
                    pe.wait_ge(Z_kept, BU * b + s1 // US)
                    if b == 0:
                        pe.wait_ge(wl_ready, 1)
                    elif b >= 2:
                        pe.wait_ge(W_normed, b - 1)
                for n in range(lo, hi):
                    f, j = n // JQ, n % JQ
                    mm = pe.matmul(psW[b % 2][:, f * BS + s0:f * BS + s1], wl_sb[:, j, f * P:(f + 1) * P],
                                   Zt[:, b, j, s0:s1], start=(j == 0), stop=(j == JQ - 1))
                if hi == FC * JQ and s1 == BS:
                    mm.then_inc(W_done, 1)

            def linear_sums(b):
                pe.wait_ge(W_squared, b + 1)
                for f in range(FC):
                    mm = pe.matmul(psS, ones[:, :], sqO[:, f * BS:(f + 1) * BS],
                                   start=(f == 0), stop=(f == FC - 1))
                mm.then_inc(W_summed, 1)

            def layer1(f, b0, b1):
                for k in range(KZ):
                    mm = pe.matmul(psH[f][:, b0 * BS:b1 * BS], w1_sb[:, k, f * P:(f + 1) * P],
                                   zT[:, k, b0 * BS:b1 * BS], start=(k == 0), stop=(k == KZ - 1))
                if b1 >= BLOCKS - 1:
                    mm.then_inc(h1_done, 1)

            pe.wait_ge(d_dense, 16)
            pe.wait_ge(d_small, 16)
            for s in range(4):
                for k in range(KD):
                    mm = pe.matmul(psB[0][:, s * E:(s + 1) * E], dense_sb[:, k, s * P:(s + 1) * P],
                                   wd_sb[:, k, :], start=(k == 0), stop=(k == KD - 1))
            mm.then_inc(x_mul, 1)
            pe.wait_ge(prep, WSI_0)
            pe.matmul(psZ[0:ROWS + 1, 0:GS * PROJ], gones_sb[0:ROWS, :], wsi_0[:, :], start=True,
                      stop=True).then_inc(wsi_summed, 1)
            pe.wait_ge(d_w1, 16)
            for f in range(K1):
                if f == 3:
                    pe.wait_ge(hd_ready, 1)
                for k in range(KD):
                    mm = pe.matmul((psA[1], psW[0], psW[1], psA[1])[f][:, :], w1_sb[:, KZ + k, f * P:(f + 1) * P],
                                   dense_sb[:, k, :], start=(k == 0), stop=(k == KD - 1))
                mm.then_inc(hd_done, 1)
                if f == 0:
                    transposes(0, 0)
                if f == 2:
                    pe.wait_ge(prep, WS_C)
                    project(0, 0)

            def step(t):
                b, n = (t - 11) // BU, (t - 11) % BU
                if 0 <= t + 2 < UNITS:
                    transposes(t + 2, (t + 2) % BU)
                if b in (0, 1):
                    linear(b, 4 * n, 4 * n + 4)
                if b == 2 and n < 6:
                    linear(b, 4 * n, 4 * n + 4 if n < 5 else FC * JQ)
                if t == UNITS + 1:
                    linear(BLOCKS - 1, 0, FC * JQ, 0, BS // 2)
                if 0 <= t - 3 < UNITS:
                    inner(t - 3, (t - 3) % BU)
                if t == 1:
                    pe.wait_ge(x_tr, 1)
                    for s in range(4):
                        mm = pe.transpose(psZ[:, s * P:(s + 1) * P], xb[:, s, :], eye_sb)
                    mm.then_inc(x_tr, 1)
                if 0 <= t < UNITS:
                    mix(t, t % BU)
                if 0 <= t + 2 < UNITS:
                    if t == -1:
                        pe.wait_ge(hd_ready, 4)
                    project(t + 2, (t + 2) % BU)
                if b in (1, 2) and n == 0:
                    linear_sums(b - 1)

            for t in range(-1, UNITS):
                step(t)
            step(UNITS)
            pe.wait_ge(y1_ready, UNITS)
            pe.wait_ge(z_ready, 2)
            layer1(0, 0, 2)
            layer1(1, 0, 2)
            step(UNITS + 1)
            linear_sums(2)
            pe.wait_ge(T_normed, UNITS)
            layer1(2, 0, 2)
            layer1(3, 0, 2)
            step(UNITS + 2)
            pe.wait_ge(z_ready, 3)
            for f in range(K1):
                layer1(f, 2, 3)
            linear(BLOCKS - 1, 0, FC * JQ, BS // 2, BS)
            pe.wait_ge(d_w2, 16)
            psL = (psZ, psW[0])

            def layer2(b0, b1):
                for k in range(K1):
                    pe.wait_ge(h1_ready, k + 1 + (K1 if b1 == BLOCKS else 0))
                    for f in range(K2):
                        mm = pe.matmul(psL[f][:, b0 * BS:b1 * BS], w2_sb[:, k, f * P:(f + 1) * P],
                                       h1T[:, k, b0 * BS:b1 * BS], start=(k == 0), stop=(k == K1 - 1))
                        if k == K1 - 1:
                            mm.then_inc(h2_done, 1)

            linear_sums(BLOCKS - 1)
            layer2(0, BLOCKS - 1)
            pe.wait_ge(z_ready, BLOCKS)
            for f in range(K1):
                layer1(f, BLOCKS - 1, BLOCKS)
            layer2(BLOCKS - 1, BLOCKS)
            for k in range(K2):
                pe.wait_ge(h2_ready, K2 + k + 1)
                mm = pe.matmul(psW[1][0:1, :], w3_c[:, k:k + 1], h2T[:, k, :], start=(k == 0), stop=(k == K2 - 1))
            mm.then_inc(y_done, 1)

        @block.scalar
        def _(act):
            def rows_out(u, m):
                lo, hi = pairs_until(m), pairs_until(m + 1)
                act.wait_ge(pair_transposed, SLOTS * (u // BU) + hi)
                if u >= BU:
                    act.wait_ge(A_done, u - BU + 2)
                act.activation(sT[:, lo * P:hi * P], psT[:, 0:(hi - lo) * P], ACT.Copy).then_inc(sT_ready, 1)

            def squares_a(u, m):
                act.wait_ge(A_done, u + 1)
                for g in range(UG):
                    last = act.activation(square[0:ROWS, m % 2, g, :], psA[m % 2][0:ROWS, g * E:(g + 1) * E], ACT.Square,
                                          accum_out=ssA[0:ROWS, m % 2, g:g + 1])
                last.then_inc(A_summed, 1)

            def deviation_a(u, m):
                act.wait_ge(A_summed, u + 1)
                if u >= 2:
                    act.wait_ge(A_recip, u - 1)
                act.activation(sdA[0:ROWS, m % 2, :], ssA[0:ROWS, m % 2, :], ACT.Sqrt, bias=eps_c[0:ROWS, :],
                               scale=1.0 / E).then_inc(A_sd, 1)

            def squares_b(u, m):
                act.wait_ge(B_done, u + 1)
                if u >= 2:
                    act.wait_ge(B_summed, u - 1)
                act.activation(sqB[:, m % 2, :], psB[m % 2][:, :], ACT.Square).then_inc(B_squared, 1)

            def deviation_b(u, m):
                act.wait_ge(B_summed, u + 1)
                if u >= 2:
                    act.wait_ge(B_recip, u - 1)
                act.activation(sdB[:, m % 2, :], ssB[:, m % 2, :], ACT.Sqrt, bias=eps_c[:, :],
                               scale=1.0 / PROJ).then_inc(B_sd, 1)

            def with_x(u, m):
                if u >= 2:
                    act.wait_ge(Z_done, u - 1)
                else:
                    act.wait_ge(xT_ready, 1)
                act.activation(Tx[:, m % 2, :, 0:1], xT[:, u * US:(u + 1) * US].rearrange("p (s o) -> p s o", o=1),
                               ACT.Copy)
                act.wait_ge(T_ready, u + 1)
                act.activation(Tx[:, m % 2, :, 1:PROJ], T[:, m % 2, :, 0:PROJ - 1], ACT.Copy).then_inc(Tx_ready, 1)

            def keep_z(u, m, part):
                act.wait_ge(Z_done, u + 1)
                b = u // BU
                for c in part:
                    src = psZ[c * PROJ:(c + 1) * PROJ, :].rearrange("p (g q j) -> p g q j", g=UG, j=JQ)
                    for q in range(4):
                        dst = Zt[q * PROJ:(q + 1) * PROJ, b, :, m * US:(m + 1) * US].rearrange(
                            "p j (g c) -> p g c j", c=GS)
                        last = act.activation(dst[:, :, c, :], src[:, :, 4 * c + q, :], ACT.Copy)
                if GS - 1 in part:
                    last.then_inc(Z_kept, 1)

            def squares_w(b):
                act.wait_ge(W_done, b + 1)
                if b >= 1:
                    act.wait_ge(W_summed, b)
                act.activation(sqO[:, :], psW[b % 2][:, :], ACT.Square).then_inc(W_squared, 1)

            def deviation_w(b):
                act.wait_ge(W_summed, b + 1)
                if b >= 1:
                    act.wait_ge(W_recip, b)
                act.activation(sdO[:, :], psS, ACT.Sqrt, bias=eps_c[:, :],
                               scale=1.0 / FLIN).then_inc(W_sd, 1)

            def scale_z(b):
                act.wait_ge(W_normed, b + 1)
                for k in range(KZ):
                    last = act.activation(zT[:, k, b * BS:(b + 1) * BS], zn[:, k, :], ACT.Identity,
                                          bias=bl_c[:, k:k + 1], scale=gl_c[:, k:k + 1])
                last.then_inc(z_ready, 1)

            act.dma_start(dense_sb[:, :, :], dense).then_inc(d_dense, 16)
            act.dma_start(w1_sb[:, :, :], w1).then_inc(d_w1, 16)
            act.dma_start(rows_sb[:, :], rows.broadcast_to([P, rows.shape[1]])).then_inc(d_rows, 16)
            act.dma_start(y1[ROWS:ROWS + 1, :, :, :], bs_rows).then_inc(d_bs, 16)
            act.wait_ge(prep, X_MV)
            act.activation(xsd[:, :], xmv[:, :, 1], ACT.Sqrt, bias=eps_c[:, :]).then_inc(x_sd, 1)
            for f in range(K1):
                if f == 1:
                    rows_out(0, 0)
                act.wait_ge(hd_done, f + 1)
                act.activation(hd[:, f, :], (psA[1], psW[0], psW[1], psA[1])[f][:, :], ACT.Identity,
                               bias=b1_c[:, f:f + 1]).then_inc(hd_ready, 1)

            def step(t):
                b, n = (t - 11) // BU, (t - 11) % BU
                if b in (1, 2) and n == 0:
                    squares_w(b - 1)
                if b in (1, 2) and n == 1:
                    deviation_w(b - 1)
                if t == UNITS + 1:
                    squares_w(2)
                if t == UNITS + 2:
                    deviation_w(2)
                if t == 2:
                    act.wait_ge(x_tr, 2)
                    act.activation(xT[:, :], psZ[:, :], ACT.Copy).then_inc(xT_ready, 1)
                if 0 <= t - 3 < UNITS:
                    with_x(t - 3, (t - 3) % BU)
                if t + 2 < UNITS:
                    rows_out(t + 2, (t + 2) % BU)
                if 0 <= t + 1 < UNITS:
                    squares_a(t + 1, (t + 1) % BU)
                    deviation_a(t + 1, (t + 1) % BU)
                if 0 <= t - 3 < UNITS:
                    keep_z(t - 3, (t - 3) % BU, (0, 1, 2))
                if 0 <= t - 1 < UNITS:
                    deviation_b(t - 1, (t - 1) % BU)
                if 0 <= t - 3 < UNITS:
                    keep_z(t - 3, (t - 3) % BU, (3,))
                if 0 <= t < UNITS:
                    squares_b(t, t % BU)
                if (b in (1, 2) and n == 1):
                    scale_z(b - 1)

            for t in range(-1, UNITS + 3):
                step(t)
            scale_z(2)

            def relu1(f, s0, s1):
                act.activation(h1T[:, f, s0:s1], h1s[:, f, s0:s1], ACT.Relu).then_inc(h1_ready, 1)

            for f in range(K1):
                act.wait_ge(h1_sum, f + 1)
                relu1(f, 0, BATCH - BS)
            squares_w(BLOCKS - 1)
            deviation_w(BLOCKS - 1)
            scale_z(BLOCKS - 1)
            psL = (psZ, psW[0])
            for s0, s1 in ((0, BATCH - BS), (BATCH - BS, BATCH)):
                for f in range(K1 if s0 else 0):
                    act.wait_ge(h1_sum, K1 + f + 1)
                    relu1(f, s0, s1)
                for f in range(K2):
                    act.wait_ge(h2_done, (K2 if s0 else 0) + f + 1)
                    act.activation(h2T[:, f, s0:s1], psL[f][:, s0:s1], ACT.Relu,
                                   bias=b2_c[:, f:f + 1]).then_inc(h2_ready, 1)

        @block.vector
        def _(dve):
            def recip_a(u, m):
                dve.wait_ge(A_sd, u + 1)
                dve.reciprocal(rA[0:ROWS, m % 2, :], sdA[0:ROWS, m % 2, :]).then_inc(A_recip, 1)

            def norm_a(u, m):
                dve.wait_ge(A_recip, u + 1)
                if u >= 2:
                    dve.wait_ge(B_done, u - 1)
                for g in range(UG):
                    last = dve.scalar_tensor_tensor(
                        out=y1[0:ROWS, m % 2, g, :], in0=psA[m % 2][0:ROWS, g * E:(g + 1) * E],
                        scalar=rA[0:ROWS, m % 2, g:g + 1], in1=gs_b[0:ROWS, :], op0=ALU.mult, op1=ALU.mult)
                last.then_inc(y1_ready, 1)

            def sums_b(u, m):
                dve.wait_ge(B_squared, u + 1)
                dve.tensor_reduce(ssB[:, m % 2, :], sqB[:, m % 2, :].rearrange("p (s j) -> p s j", j=PROJ),
                                  AX, ALU.add).then_inc(B_summed, 1)

            def recip_b(u, m):
                dve.wait_ge(B_sd, u + 1)
                dve.reciprocal(rB[:, m % 2, :], sdB[:, m % 2, :]).then_inc(B_recip, 1)

            def norm_b(u, m):
                dve.wait_ge(B_recip, u + 1)
                if u >= 2:
                    dve.wait_ge(Z_done, u - 1)
                dve.tensor_tensor(T[:, m % 2, :, :], psB[m % 2][:, :].rearrange("p (s j) -> p s j", j=PROJ),
                                  rB[:, m % 2, :].rearrange("p (s o) -> p s o", o=1).broadcast_to([P, US, PROJ]),
                                  ALU.mult).then_inc(T_normed, 1)

            def scale_b(u, m):
                dve.wait_ge(T_normed, u + 1)
                dve.tensor_tensor(T[:, m % 2, :, :], T[:, m % 2, :, :],
                                  gsi_b.rearrange("p (o j) -> p o j", o=1).broadcast_to([P, US, PROJ]),
                                  ALU.mult).then_inc(T_scaled, 1)

            def shift_b(u, m):
                dve.wait_ge(T_scaled, u + 1)
                dve.tensor_tensor(T[:, m % 2, :, :], T[:, m % 2, :, :],
                                  bsi_b.rearrange("p (o j) -> p o j", o=1).broadcast_to([P, US, PROJ]),
                                  ALU.add).then_inc(T_ready, 1)

            def recip_w(b):
                dve.wait_ge(W_sd, b + 1)
                dve.reciprocal(rO[:, :], sdO[:, :]).then_inc(W_recip, 1)

            def norm_w(b):
                dve.wait_ge(W_recip, b + 1)
                if b >= 1:
                    dve.wait_ge(z_ready, b)
                dve.tensor_tensor(zn[:, :, :], psW[b % 2][:, 0:KZ * BS].rearrange("p (k s) -> p k s", k=KZ),
                                  rO[:, :].rearrange("p (o s) -> p o s", o=1).broadcast_to([P, KZ, BS]),
                                  ALU.mult).then_inc(W_normed, 1)

            dve.memset(eps_c[:, :], EPS).then_inc(prep, 1)
            dve.memset(ones[:, :], 1.0).then_inc(prep, 1)
            dve.wait_ge(d_small, 16)
            dve.tensor_reduce(means[0:ROWS, 0:1], wsi_sb[0:ROWS, :], AX, ALU.add).then_inc(prep, 1)
            dve.tensor_reduce(means[:, 1:2], ws_sb, AX, ALU.add).then_inc(prep, 1)
            dve.wait_ge(prep, 4)
            dve.tensor_scalar(means[0:ROWS, 2:3], means[0:ROWS, 0:1], -1.0 / PROJ, None, ALU.mult)
            dve.tensor_scalar(means[:, 3:4], means[:, 1:2], -1.0 / E, None, ALU.mult).then_inc(prep, 1)
            dve.wait_ge(prep, 5)
            dve.scalar_tensor_tensor(out=wsi_0[:, :], in0=wsim_sb[0:ROWS, :], scalar=means[0:ROWS, 2:3],
                                     in1=wsi_sb[0:ROWS, :], op0=ALU.mult, op1=ALU.add).then_inc(prep, 1)
            dve.scalar_tensor_tensor(out=ws_c[:, :], in0=wsm_sb, scalar=means[:, 3:4],
                                     in1=ws_sb, op0=ALU.mult, op1=ALU.add).then_inc(prep, 1)
            dve.wait_ge(wsi_summed, 1)
            dve.tensor_copy(wsi_c[:, :], psZ[0:ROWS + 1, 0:GS * PROJ]).then_inc(prep, 1)
            dve.wait_ge(x_mul, 1)
            for s in range(4):
                last = dve.bn_stats(xstat[:, s, :], psB[0][:, s * E:(s + 1) * E])
            last.then_inc(prep, 1)
            dve.wait_ge(prep, 9)
            for s in range(4):
                last = dve.bn_aggr(xmv[:, s, :], xstat[:, s, :])
            last.then_inc(prep, 1)
            dve.wait_ge(x_sd, 1)
            dve.reciprocal(xr[:, :], xsd[:, :]).then_inc(prep, 1)
            dve.wait_ge(prep, 11)
            for s in range(4):
                last = dve.tensor_scalar(xn[:, s, :], psB[0][:, s * E:(s + 1) * E], xmv[:, s, 0:1], xr[:, s:s + 1],
                                         ALU.subtract, ALU.mult)
            last.then_inc(prep, 1)
            dve.wait_ge(prep, 12)
            dve.wait_ge(d_rows, 16)
            dve.tensor_tensor(xg[:, :, :], xn[:, :, :],
                              gd_b.rearrange("p (o e) -> p o e", o=1).broadcast_to([P, 4, E]),
                              ALU.mult).then_inc(prep, 1)
            dve.wait_ge(prep, 13)
            dve.tensor_tensor(xb[:, :, :], xg[:, :, :],
                              bd_b.rearrange("p (o e) -> p o e", o=1).broadcast_to([P, 4, E]),
                              ALU.add).then_inc(x_tr, 1)

            dve.wait_ge(d_wl, 16)
            dve.tensor_reduce(wl_mean[:, 0:JQ], wl_sb[:, :, :], AX, ALU.add).then_inc(prep, 1)
            dve.wait_ge(prep, 14)
            dve.tensor_scalar(wl_mean[:, JQ:2 * JQ], wl_mean[:, 0:JQ], 1.0 / FLIN, None,
                              ALU.mult).then_inc(prep, 1)
            dve.wait_ge(prep, 15)

            def center_wl(j):
                last = dve.tensor_scalar(wl_sb[:, j, :], wl_sb[:, j, :], wl_mean[:, JQ + j:JQ + j + 1], None,
                                         ALU.subtract)
                if j == JQ - 1:
                    last.then_inc(wl_ready, 1)

            def step(t):
                if 0 <= t - 2 < UNITS:
                    norm_b(t - 2, (t - 2) % BU)
                if 0 <= t < UNITS:
                    recip_a(t, t % BU)
                    norm_a(t, t % BU)
                if 0 <= t - 2 < UNITS:
                    scale_b(t - 2, (t - 2) % BU)
                if 0 <= t - 1 < UNITS:
                    sums_b(t - 1, (t - 1) % BU)
                if 0 <= t - 2 < UNITS:
                    shift_b(t - 2, (t - 2) % BU)
                if 0 <= t - 1 < UNITS:
                    recip_b(t - 1, (t - 1) % BU)
                if 0 <= t < JQ:
                    center_wl(t)
                b, n = (t - 11) // BU, (t - 11) % BU
                if b in (1, 2) and n == 1:
                    recip_w(b - 1)
                    norm_w(b - 1)

            for t in range(0, UNITS + 2):
                step(t)
            recip_w(2)
            norm_w(2)

            def add_dense(f, s0, s1):
                dve.wait_ge(h1_done, (K1 if s0 else 0) + f + 1)
                dve.tensor_tensor(h1s[:, f, s0:s1], psH[f][:, s0:s1], hd[:, f, s0:s1], ALU.add).then_inc(h1_sum, 1)

            for f in range(K1):
                add_dense(f, 0, BATCH - BS)
            recip_w(BLOCKS - 1)
            norm_w(BLOCKS - 1)
            for f in range(K1):
                add_dense(f, BATCH - BS, BATCH)
            dve.wait_ge(y_done, 1)
            dve.tensor_copy(y_sb[:, :], psW[1][0:1, :]).then_inc(y_ready, 1)


def kernel(**inputs):
    import numpy as np
    import concourse.bacc as bacc
    from concourse.bass_utils import run_bass_kernel_spmd

    x = {k: np.asarray(v) for k, v in inputs.items()}
    tables = [x[f"tbl_{n}"] for n in range(NSP)]

    def chunks(a):
        return np.ascontiguousarray(a.reshape(-1, 2, ROWS).transpose(1, 0, 2).reshape(2, PAIRS, P)
                                    .transpose(2, 1, 0).reshape(P, 2 * PAIRS))

    def on_partitions(a):
        return np.ascontiguousarray(a.reshape(-1, P, a.shape[1]).transpose(1, 0, 2))

    def diagonal(a, n):
        d = np.zeros((n, a.shape[0], n, a.shape[1]), a.dtype)
        for i in range(n):
            d[i, :, i, :] = a
        return d.reshape(n * a.shape[0], n * a.shape[1])

    starts = np.cumsum([0] + [t.shape[0] for t in tables[:-1]]).astype(np.int32)
    gather_ones = np.eye(ROWS, ROWS + 1, dtype=np.float32)
    gather_ones[:, ROWS] = 1.0
    q, i, j = np.meshgrid(np.arange(4), np.arange(1, PROJ + 1), np.arange(JQ), indexing="ij")
    j = q * JQ + j
    pairs = PROJ * (PROJ + 1) // 2
    at = np.where(i > j, i * (i - 1) // 2 + j, pairs).reshape(P, JQ)
    wl = x["L0_rec_Wl"].T
    wl = np.concatenate([wl, np.zeros((1, FLIN), wl.dtype)])[at]
    w1 = x["W_top1"]
    cols = np.concatenate([x["b_top1"].reshape(K1, P), x["b_top2"].reshape(K2, P), x["W_top3"].reshape(K2, P),
                           x["L0_rec_gl"][:FOUT].reshape(KZ, P), x["L0_rec_bl"][:FOUT].reshape(KZ, P)]).T

    def full(a):
        return np.concatenate([a, np.zeros((P - a.shape[0], a.shape[1]), a.dtype)])

    arrays = {
        "table": np.concatenate(tables, axis=0),
        "ids": np.stack([chunks(x["ids"]), chunks(np.broadcast_to(starts, (BATCH, NSP)))], axis=1),
        "small": np.concatenate([full(a) for a in (
            on_partitions(x["L0_rec_Wd"].T).reshape(P, KD * E),
            diagonal(x["L0_rec_Ws"].T, 2), diagonal(np.ones((DSP, E), np.float32), 2),
            diagonal(x["L0_rec_Wsi"].T, GS), diagonal(np.ones((NSP, PROJ), np.float32), GS),
            gather_ones, np.eye(P, dtype=np.float32), cols)], axis=1),
        "rows": np.concatenate([x[f"L0_rec_{n}"] for n in ("gs", "gd", "bd", "gsi", "bsi")])[None, :],
        "bs_rows": np.ascontiguousarray(np.broadcast_to(x["L0_rec_bs"], (1, 2, UG, E))),
        "dense": on_partitions(x["r_dense_t"].T),
        "wl": wl,
        "w1": on_partitions(np.concatenate([w1[:FOUT], w1[FLIN:]])),
        "w2": on_partitions(x["W_top2"]),
    }
    nc = bacc.Bacc("TRN2", target_bir_lowering=False, num_devices=1)
    args = [nc.dram_tensor(f"in_{n}", a.shape, mybir.dt.from_np(a.dtype), kind="ExternalInput").ap()
            for n, a in arrays.items()]
    out = nc.dram_tensor("out_y", (BATCH, 1), F32, kind="ExternalOutput").ap()
    tower(nc, *args, out)
    r = run_bass_kernel_spmd(nc, [{f"in_{n}": a for n, a in arrays.items()}], core_ids=[0])
    return r.results[0]["out_y"]
```

```python
from contextlib import ExitStack

import concourse.bass as bass
from concourse import mybir

F32 = mybir.dt.float32
I32 = mybir.dt.int32
ALU = mybir.AluOpType
ACT = mybir.ActivationFunctionType
AX = mybir.AxisListType.X

P = 128
BATCH, NSP, DSP = 512, 26, 64
E, PROJ = 128, 32
FLIN, FOUT = 512, 384
DENSE, H1, H2 = 256, 512, 256
EPS = 1e-5

GS = 4
ROWS = GS * NSP
UG = 4
US = UG * GS
UNITS = BATCH // US
BU = 8
BS = BU * US
BLOCKS = BATCH // BS
PAIRS = BATCH * NSP // P // 2
SLOTS = PAIRS // BLOCKS
JQ = PROJ // 4
KD, KZ, K1, K2 = DENSE // P, FOUT // P, H1 // P, H2 // P
FC = FLIN // P
FIRST_W = BU + 3
FEW = 5
GATHER_LEAD = 5
WL_PIECES = 4
SMALL = [0]
for width in (KD * E, 2 * E, 2 * E, GS * PROJ, GS * PROJ, ROWS + 1, P, K1 + 2 * K2 + 2 * KZ):
    SMALL.append(SMALL[-1] + width)


def pairs_until(m):
    return -(-(m * 2 * ROWS) // P)


def on_pool(u):
    return u % 4 == 3 and u < UNITS - 2


def shifts(u):
    return sum(on_pool(v) == on_pool(u) for v in range(u + 1))


def tower(nc, table, ids, small, rows, bs_rows, dense, wl, w1, w2, out):
    with ExitStack() as ctx:
        def sb(name, shape, dt=F32):
            return ctx.enter_context(nc.sbuf_tensor(name, shape, dt))

        def ps(name):
            return ctx.enter_context(nc.psum_tensor(name, [P, 512], F32))

        def sem(name):
            return ctx.enter_context(nc.semaphore(name))

        ids_sb = sb("ids_sb", [P, 2, 2 * PAIRS], I32)
        row_id = sb("row_id", [P, 2 * PAIRS], I32)
        small_sb = sb("small_sb", [P, SMALL[-1]])
        (wd_f, ws_sb, wsm_sb, wsi_sb, wsim_sb, gones_sb, eye_sb, cols_sb) = (
            small_sb[:, lo:hi] for lo, hi in zip(SMALL[:-1], SMALL[1:]))
        wd_sb = wd_f.rearrange("p (k e) -> p k e", k=KD)
        b1_c = cols_sb[:, 0:K1]
        b2_c = cols_sb[:, K1:K1 + K2]
        w3_c = cols_sb[:, K1 + K2:K1 + 2 * K2]
        gl_c = cols_sb[:, K1 + 2 * K2:K1 + 2 * K2 + KZ]
        bl_c = cols_sb[:, K1 + 2 * K2 + KZ:K1 + 2 * K2 + 2 * KZ]
        rows_sb = sb("rows_sb", [P, 3 * E + 2 * PROJ])
        gs_b, gd_b, bd_b = (rows_sb[:, n * E:(n + 1) * E] for n in range(3))
        gsi_b = rows_sb[:, 3 * E:3 * E + PROJ]
        bsi_b = rows_sb[:, 3 * E + PROJ:3 * E + 2 * PROJ]
        ones = sb("ones", [P, P])
        eps_c = sb("eps_c", [P, 1])
        first_root = sb("first_root", [P, 1])
        means = sb("means", [P, 4])
        ws_c = sb("ws_c", [P, 2 * E])
        wsi_0 = sb("wsi_0", [ROWS, GS * PROJ])
        wsi_c = sb("wsi_c", [ROWS + 1, GS * PROJ])
        dense_sb = sb("dense_sb", [P, KD, BATCH])
        wl_sb = sb("wl_sb", [P, JQ, FLIN])
        wl_neg = sb("wl_neg", [P, FLIN])
        wl_mean = sb("wl_mean", [P, JQ])
        w1_sb = sb("w1_sb", [P, KZ + KD, H1])
        w2_sb = sb("w2_sb", [P, K1, H2])

        xstat = sb("xstat", [P, 4, 6])
        xmv = sb("xmv", [P, 4, 2])
        xsd = sb("xsd", [P, 4])
        xr = sb("xr", [P, 4])
        xn = sb("xn", [P, 4, E])
        xg = sb("xg", [P, 4, E])
        xb = sb("xb", [P, 4, E])
        xT = sb("xT", [P, BATCH])

        g_sb = sb("g_sb", [P, SLOTS, P])
        sT = sb("sT", [P, SLOTS * P])
        square = sb("square", [P, 2, UG, E])
        ssA = sb("ssA", [P, 2, UG])
        sdA = sb("sdA", [P, 2, UG])
        rA = sb("rA", [P, 2, UG])
        y1 = sb("y1", [ROWS + 1, 2, UG, E])
        sqB = sb("sqB", [P, 2, US * PROJ])
        ssB = sb("ssB", [P, 2, US])
        sdB = sb("sdB", [P, 2, US])
        rB = sb("rB", [P, 2, US])
        T = sb("T", [P, 2, US, 1 + PROJ])
        Zt = sb("Zt", [P, BLOCKS, JQ, BS])
        sqO = sb("sqO", [P, FC * BS])
        sdO = sb("sdO", [P, BS])
        rO = sb("rO", [P, BS])
        zn = sb("zn", [P, KZ, BS])
        zT = sb("zT", [P, KZ, BATCH])
        hd = sb("hd", [P, K1, BATCH])
        h1T = sb("h1T", [P, K1, BATCH])
        h2T = sb("h2T", [P, K2, BATCH])
        y_sb = sb("y_sb", [1, BATCH])

        psT, psZ = ps("psT"), ps("psZ")
        psW = [ps("psW0"), ps("psW1")]
        psS = [w[:, KZ * BS:(KZ + 1) * BS] for w in psW]
        psA = [ps("psA0"), ps("psA1")]
        psB = [ps("psB0"), ps("psB1")]
        psX = psW[0]
        psD = [psW[1], psW[0], psW[1], psW[0]]
        psH = [psW[0], psA[0], psB[0], psA[1]]

        d_ids, d_small, d_rows, d_bs, d_dense, d_wl, d_w1d, d_w1, d_w2, d_out = (
            sem(n) for n in ("d_ids", "d_small", "d_rows", "d_bs", "d_dense", "d_wl", "d_w1d", "d_w1", "d_w2", "d_out"))
        gathered = [sem(f"gathered{n}") for n in range(SLOTS)]
        ids_added = sem("ids_added")
        prep = sem("prep")
        wsi_summed = sem("wsi_summed")
        x_mul, x_sd, x_tr = sem("x_mul"), sem("x_sd"), sem("x_tr")
        xT_ready = sem("xT_ready")
        wl_summed, wl_ready = sem("wl_summed"), sem("wl_ready")
        pair_transposed, sT_ready = sem("pair_transposed"), sem("sT_ready")
        A_done, A_summed, A_sd, A_recip, y1_ready = (sem(n) for n in ("A_done", "A_summed", "A_sd", "A_recip",
                                                                      "y1_ready"))
        B_done, B_squared, B_summed, B_sd, B_recip = (sem(n) for n in ("B_done", "B_squared", "B_summed", "B_sd",
                                                                       "B_recip"))
        T_normed, T_scaled, T_dve, T_pool, x_in = (sem(n) for n in ("T_normed", "T_scaled", "T_dve", "T_pool", "x_in"))
        T_ready = {False: T_dve, True: T_pool}
        Z_done, Z_kept = sem("Z_done"), sem("Z_kept")
        W_done, W_squared, W_summed, W_sd, W_recip, W_normed, z_ready = (
            sem(n) for n in ("W_done", "W_squared", "W_summed", "W_sd", "W_recip", "W_normed", "z_ready"))
        h1_done, h1_ready, h2_done, h2_ready, y_done, y_copied = (
            sem(n) for n in ("h1_done", "h1_ready", "h2_done", "h2_ready", "y_done", "y_copied"))
        hd_done, hd_ready = sem("hd_done"), sem("hd_ready")
        WSI_0, WS_C, WSI_C, X_STAT, X_MV, X_R, X_N, X_G = range(6, 14)

        block = ctx.enter_context(nc.Block())

        @block.sync
        def _(sp):
            sp.dma_start(ids_sb[:, :, :], ids).then_inc(d_ids, 16)
            sp.dma_start(small_sb[:, :], small).then_inc(d_small, 16)
            sp.wait_ge(gathered[1], 32)
            sp.dma_start(w1_sb[:, KZ:, :], w1[:, KZ:, :]).then_inc(d_w1d, 16)
            for n in range(WL_PIECES):
                sp.wait_ge(gathered[2 + n], 32)
                if n:
                    sp.wait_ge(d_wl, 16 * n)
                js = slice(n * JQ // WL_PIECES, (n + 1) * JQ // WL_PIECES)
                sp.dma_start(wl_sb[:, js, :], wl[:, js, :]).then_inc(d_wl, 16)
            sp.wait_ge(gathered[2 + WL_PIECES], 32)
            sp.dma_start(w1_sb[:, 0:KZ, :], w1[:, 0:KZ, :]).then_inc(d_w1, 16)
            sp.wait_ge(gathered[SLOTS - 1], 32)
            sp.dma_start(w2_sb[:, :, :], w2).then_inc(d_w2, 16)
            sp.wait_ge(y_copied, BLOCKS)
            sp.dma_start(out.rearrange("b o -> o b"), y_sb[:, :]).then_inc(d_out, 16)
            sp.wait_ge(d_out, 16)

        @block.gpsimd
        def _(pool):
            pool.wait_ge(d_ids, 16)
            pool.tensor_tensor(row_id[:, :], ids_sb[:, 0, :], ids_sb[:, 1, :], ALU.add).then_inc(ids_added, 1)
            pool.wait_ge(ids_added, 1)
            def gathers(lo, hi):
                for k in range(lo, hi):
                    if k >= SLOTS:
                        pool.wait_ge(pair_transposed, k - SLOTS + 1)
                    for h in range(2):
                        pool.indirect_dma_start(
                            g_sb[:, k % SLOTS, h * DSP:(h + 1) * DSP], None, table,
                            bass.IndirectOffsetOnAxis(row_id[:, 2 * k + h:2 * k + h + 1], 0),
                        ).then_inc(gathered[k % SLOTS], 16)

            def shift_b(u, m):
                pool.wait_ge(T_scaled, u + 1)
                pool.tensor_tensor(T[:, m % 2, :, 1:], T[:, m % 2, :, 1:],
                                   bsi_b.rearrange("p (o j) -> p o j", o=1).broadcast_to([P, US, PROJ]),
                                   ALU.add).then_inc(T_pool, 1)

            done = 0
            for u in range(UNITS):
                if on_pool(u):
                    ahead = min(PAIRS, pairs_until(u + 1 + GATHER_LEAD))
                    gathers(done, ahead)
                    done = ahead
                    shift_b(u, u % BU)

        @block.tensor
        def _(pe):
            def transposes(u, m):
                if u:
                    pe.wait_ge(sT_ready, u)
                for n, k in enumerate(range(pairs_until(m), pairs_until(m + 1))):
                    pe.wait_ge(gathered[k], 32 * (u // BU + 1))
                    pe.transpose(psT[:, n * P:(n + 1) * P], g_sb[:, k, :], eye_sb).then_inc(pair_transposed, 1)

            def project(u, m):
                pe.wait_ge(sT_ready, u + 1)
                if u >= 2:
                    pe.wait_ge(y1_ready, u - 1)
                for g in range(2):
                    mm = pe.matmul(psA[m % 2][0:ROWS, g * 2 * E:(g + 1) * 2 * E],
                                   sT[:, (2 * m + g) * ROWS:(2 * m + g + 1) * ROWS], ws_c[:, :],
                                   start=True, stop=True)
                mm.then_inc(A_done, 1)

            def mix(u, m):
                pe.wait_ge(y1_ready, u + 1)
                if u == 0:
                    pe.wait_ge(prep, WSI_C)
                    pe.wait_ge(d_bs, 16)
                if u >= 2:
                    pe.wait_ge(T_normed, u - 1)
                for g in range(UG):
                    mm = pe.matmul(psB[m % 2][:, g * P:(g + 1) * P], y1[:, m % 2, g, :], wsi_c[:, :],
                                   start=True, stop=True)
                mm.then_inc(B_done, 1)

            def inner(u, m):
                pe.wait_ge(T_ready[on_pool(u)], shifts(u))
                pe.wait_ge(x_in, u + 1)
                if u >= 2:
                    pe.wait_ge(Z_kept, u - 1)
                for s in range(US):
                    mm = pe.matmul(psZ[(m % 2) * PROJ:(m % 2 + 1) * PROJ, s * PROJ:(s + 1) * PROJ],
                                   T[:, m % 2, s, 1:1 + PROJ], T[:, m % 2, s, 0:PROJ], start=True, stop=True)
                mm.then_inc(Z_done, 1)

            def linear(b, lo, hi, s0=0, s1=BS):
                if lo == 0:
                    pe.wait_ge(Z_kept, BU * b + s1 // US)
                    if b == 0:
                        pe.wait_ge(wl_ready, 1)
                        pe.wait_ge(hd_ready, K1)
                    if b == 2:
                        pe.wait_ge(y_copied, 1)
                    if b == 3:
                        pe.wait_ge(W_normed, 2)
                for n in range(lo, hi):
                    f, j = n // JQ, n % JQ
                    mm = pe.matmul(psW[b % 2][:, f * BS + s0:f * BS + s1], wl_sb[:, j, f * P:(f + 1) * P],
                                   Zt[:, b, j, s0:s1], start=(j == 0), stop=(j == JQ - 1))
                if hi == FC * JQ and s1 == BS:
                    mm.then_inc(W_done, 1)

            def linear_sums(b):
                pe.wait_ge(W_squared, b + 1)
                for f in range(FC):
                    mm = pe.matmul(psS[b % 2], ones[:, :], sqO[:, f * BS:(f + 1) * BS],
                                   start=(f == 0), stop=(f == FC - 1))
                mm.then_inc(W_summed, 1)

            def dense_part(f, k):
                if f == 0 and k == 0:
                    pe.wait_ge(d_w1d, 16)
                if f == 1 and k == 0:
                    pe.wait_ge(prep, X_N)
                if f >= 2 and k == 0:
                    pe.wait_ge(hd_ready, f - 1)
                mm = pe.matmul(psD[f][:, :], w1_sb[:, KZ + k, f * P:(f + 1) * P], dense_sb[:, k, :],
                               start=(k == 0), stop=(k == KD - 1))
                if k == KD - 1:
                    mm.then_inc(hd_done, 1)

            def layer1(b, lo, hi):
                if lo == 0:
                    pe.wait_ge(z_ready, b + 1)
                    if b == 0:
                        pe.wait_ge(d_w1, 16)
                    if b == 1:
                        pe.wait_ge(y1_ready, UNITS - 1)
                    if b == 2:
                        pe.wait_ge(T_normed, UNITS - 1)
                    if b == 3:
                        pe.wait_ge(y1_ready, UNITS)
                for f in range(lo, hi):
                    pe.matmul(psH[b][:, f * BS:(f + 1) * BS], eye_sb, hd[:, f, b * BS:(b + 1) * BS],
                              start=True, stop=False)
                    for k in range(KZ):
                        mm = pe.matmul(psH[b][:, f * BS:(f + 1) * BS], w1_sb[:, k, f * P:(f + 1) * P],
                                       zT[:, k, b * BS:(b + 1) * BS], start=False, stop=(k == KZ - 1))
                if hi == K1:
                    mm.then_inc(h1_done, 1)

            def layer2(b):
                pe.wait_ge(h1_ready, b + 1)
                if b == 0:
                    pe.wait_ge(d_w2, 16)
                for f in range(K2):
                    for k in range(K1):
                        mm = pe.matmul(psH[b][:, f * BS:(f + 1) * BS], w2_sb[:, k, f * P:(f + 1) * P],
                                       h1T[:, k, b * BS:(b + 1) * BS], start=(k == 0), stop=(k == K1 - 1))
                mm.then_inc(h2_done, 1)

            def output(b):
                pe.wait_ge(h2_ready, b + 1)
                for k in range(K2):
                    mm = pe.matmul(psH[b][0:1, K2 * BS:(K2 + 1) * BS], w3_c[:, k:k + 1], h2T[:, k, b * BS:(b + 1) * BS],
                                   start=(k == 0), stop=(k == K2 - 1))
                mm.then_inc(y_done, 1)

            pe.wait_ge(d_dense, 16)
            pe.wait_ge(d_small, 16)
            for s in range(4):
                for k in range(KD):
                    mm = pe.matmul(psX[:, s * E:(s + 1) * E], dense_sb[:, k, s * P:(s + 1) * P],
                                   wd_sb[:, k, :], start=(k == 0), stop=(k == KD - 1))
            mm.then_inc(x_mul, 1)
            transposes(0, 0)
            pe.wait_ge(prep, WSI_0)
            pe.matmul(psZ[0:ROWS + 1, 0:GS * PROJ], gones_sb[0:ROWS, :], wsi_0[:, :], start=True,
                      stop=True).then_inc(wsi_summed, 1)
            pe.wait_ge(prep, WS_C)
            project(0, 0)

            def step(t):
                b, n = (t - FIRST_W) // BU, (t - FIRST_W) % BU
                if b in (0, 1):
                    linear(b, 4 * n, 4 * n + 4)
                if t == 26:
                    output(0)
                if b == 2 and n < 5:
                    ends = (0, 4, 8, 12, 22, FC * JQ)
                    linear(b, ends[n], ends[n + 1])
                if 0 <= t - 3 < UNITS:
                    inner(t - 3, (t - 3) % BU)
                if FEW <= t and t + 2 < UNITS:
                    transposes(t + 2, (t + 2) % BU)
                if t == 2:
                    pe.wait_ge(x_tr, 1)
                    for s in range(4):
                        mm = pe.transpose(psZ[:, s * P:(s + 1) * P], xb[:, s, :], eye_sb)
                    mm.then_inc(x_tr, 1)
                if b in (1, 2) and n == 1:
                    linear_sums(b - 1)
                if 0 <= t < UNITS:
                    mix(t, t % BU)
                if t < FEW:
                    transposes(t + 2, (t + 2) % BU)
                if 2 <= t < 2 + K1 * KD:
                    dense_part((t - 2) // KD, (t - 2) % KD)
                if 0 <= t + 2 < UNITS:
                    project(t + 2, (t + 2) % BU)
                if t in (23, 24):
                    layer1(0, K1 // 2 * (t - 23), K1 // 2 * (t - 22))
                if t == 25:
                    layer2(0)

            for t in range(-1, UNITS):
                step(t)
            layer1(1, 0, 2)
            linear_sums(2)
            step(UNITS)
            layer1(1, 2, K1)
            step(UNITS + 1)
            step(UNITS + 2)
            layer2(1)
            linear(BLOCKS - 1, 0, FC * JQ)
            output(1)
            linear_sums(BLOCKS - 1)
            layer1(2, 0, K1)
            layer1(BLOCKS - 1, 0, K1)
            layer2(2)
            layer2(BLOCKS - 1)
            output(2)
            output(BLOCKS - 1)

        @block.scalar
        def _(act):
            def rows_out(u, m):
                lo, hi = pairs_until(m), pairs_until(m + 1)
                act.wait_ge(pair_transposed, SLOTS * (u // BU) + hi)
                if u >= BU:
                    act.wait_ge(A_done, u - BU + 2)
                act.activation(sT[:, lo * P:hi * P], psT[:, 0:(hi - lo) * P], ACT.Copy).then_inc(sT_ready, 1)

            def squares_a(u, m):
                act.wait_ge(A_done, u + 1)
                for g in range(UG):
                    last = act.activation(square[0:ROWS, m % 2, g, :], psA[m % 2][0:ROWS, g * E:(g + 1) * E], ACT.Square,
                                          accum_out=ssA[0:ROWS, m % 2, g:g + 1])
                last.then_inc(A_summed, 1)

            def deviation_a(u, m):
                act.wait_ge(A_summed, u + 1)
                if u >= 2:
                    act.wait_ge(A_recip, u - 1)
                act.activation(sdA[0:ROWS, m % 2, :], ssA[0:ROWS, m % 2, :], ACT.Sqrt, bias=eps_c[0:ROWS, :],
                               scale=1.0 / E).then_inc(A_sd, 1)

            def squares_b(u, m):
                act.wait_ge(B_done, u + 1)
                if u >= 2:
                    act.wait_ge(B_summed, u - 1)
                act.activation(sqB[:, m % 2, :], psB[m % 2][:, :], ACT.Square).then_inc(B_squared, 1)

            def deviation_b(u, m):
                act.wait_ge(B_summed, u + 1)
                if u >= 2:
                    act.wait_ge(B_recip, u - 1)
                act.activation(sdB[:, m % 2, :], ssB[:, m % 2, :], ACT.Sqrt, bias=eps_c[:, :],
                               scale=1.0 / PROJ).then_inc(B_sd, 1)

            def enter_x(u, m):
                if u >= 2:
                    act.wait_ge(Z_done, u - 1)
                if u == 0:
                    act.wait_ge(xT_ready, 1)
                act.activation(T[:, m % 2, :, 0:1], xT[:, u * US:(u + 1) * US].rearrange("p (s o) -> p s o", o=1),
                               ACT.Copy).then_inc(x_in, 1)

            def keep_z(u, m):
                act.wait_ge(Z_done, u + 1)
                src = psZ[(m % 2) * PROJ:(m % 2 + 1) * PROJ, :].rearrange("p (s q j) -> p s q j", s=US, j=JQ)
                for q in range(4):
                    dst = Zt[q * PROJ:(q + 1) * PROJ, u // BU, :, m * US:(m + 1) * US].rearrange("p j s -> p s j")
                    last = act.activation(dst, src[:, :, q, :], ACT.Copy)
                last.then_inc(Z_kept, 1)

            def sum_wl(j):
                act.wait_ge(d_wl, 16 * (j * WL_PIECES // JQ + 1))
                if j:
                    act.wait_ge(wl_summed, j)
                act.activation(wl_neg[:, :], wl_sb[:, j, :], ACT.Copy, scale=-1.0 / FLIN,
                               accum_out=wl_mean[:, j:j + 1]).then_inc(wl_summed, 1)

            def squares_w(b):
                act.wait_ge(W_done, b + 1)
                if b >= 1:
                    act.wait_ge(W_summed, b)
                act.activation(sqO[:, :], psW[b % 2][:, :], ACT.Square).then_inc(W_squared, 1)

            def deviation_w(b):
                act.wait_ge(W_summed, b + 1)
                if b >= 1:
                    act.wait_ge(W_recip, b)
                act.activation(sdO[:, :], psS[b % 2], ACT.Sqrt, bias=eps_c[:, :],
                               scale=1.0 / FLIN).then_inc(W_sd, 1)

            def scale_z(b):
                act.wait_ge(W_normed, b + 1)
                for k in range(KZ):
                    last = act.activation(zT[:, k, b * BS:(b + 1) * BS], zn[:, k, :], ACT.Identity,
                                          bias=bl_c[:, k:k + 1], scale=gl_c[:, k:k + 1])
                last.then_inc(z_ready, 1)

            act.dma_start(dense_sb[:, :, :], dense).then_inc(d_dense, 16)
            act.dma_start(rows_sb[:, :], rows.broadcast_to([P, rows.shape[1]])).then_inc(d_rows, 16)
            act.dma_start(y1[ROWS:ROWS + 1, :, :, :], bs_rows).then_inc(d_bs, 16)
            act.wait_ge(prep, 1)
            act.activation(first_root[:, :], eps_c[:, :], ACT.Sqrt)
            rows_out(0, 0)

            def relu1(b):
                act.wait_ge(h1_done, b + 1)
                act.activation(h1T[:, :, b * BS:(b + 1) * BS],
                               psH[b][:, :].rearrange("p (k s) -> p k s", k=K1), ACT.Relu).then_inc(h1_ready, 1)

            def relu2(b):
                act.wait_ge(h2_done, b + 1)
                for f in range(K2):
                    last = act.activation(h2T[:, f, b * BS:(b + 1) * BS], psH[b][:, f * BS:(f + 1) * BS], ACT.Relu,
                                          bias=b2_c[:, f:f + 1])
                last.then_inc(h2_ready, 1)

            def step(t):
                b, n = (t - FIRST_W) // BU, (t - FIRST_W) % BU
                if 0 <= t + 1 < UNITS:
                    squares_a(t + 1, (t + 1) % BU)
                    deviation_a(t + 1, (t + 1) % BU)
                if b in (1, 2) and n == 2:
                    deviation_w(b - 1)
                if t == -1:
                    act.wait_ge(prep, X_MV)
                    act.activation(xsd[:, :], xmv[:, :, 1], ACT.Sqrt, bias=eps_c[:, :]).then_inc(x_sd, 1)
                if not 0 <= t < FEW and t + 2 < UNITS:
                    rows_out(t + 2, (t + 2) % BU)
                if UNITS <= t < UNITS + 2:
                    enter_x(t - 2, (t - 2) % BU)
                if t == UNITS:
                    deviation_b(t - 1, (t - 1) % BU)
                    deviation_w(2)
                if 0 <= t - 3 < UNITS:
                    keep_z(t - 3, (t - 3) % BU)
                if 0 <= t - 1 < UNITS - 1:
                    deviation_b(t - 1, (t - 1) % BU)
                if 0 <= t < UNITS:
                    squares_b(t, t % BU)
                if 0 <= t < FEW:
                    rows_out(t + 2, (t + 2) % BU)
                if t == 2:
                    act.wait_ge(x_tr, 2)
                    act.activation(xT[:, :], psZ[:, :], ACT.Copy).then_inc(xT_ready, 1)
                if 0 <= t - 2 < UNITS - 2:
                    enter_x(t - 2, (t - 2) % BU)
                if 0 <= t < JQ:
                    sum_wl(t)
                if t > 2 and (t - 2) % KD == 0 and (t - 2) // KD <= K1:
                    f = (t - 2) // KD - 1
                    act.wait_ge(hd_done, f + 1)
                    act.activation(hd[:, f, :], psD[f][:, :], ACT.Identity, bias=b1_c[:, f:f + 1]).then_inc(hd_ready, 1)
                if b in (1, 2) and n == 0:
                    squares_w(b - 1)
                if b in (1, 2) and n == 3:
                    scale_z(b - 1)
                if t == 24:
                    relu1(0)
                if t == 25:
                    relu2(0)
                if t == UNITS - 1:
                    squares_w(2)

            for t in range(-1, UNITS + 1):
                step(t)
            relu1(1)
            step(UNITS + 1)
            step(UNITS + 2)
            scale_z(2)
            relu2(1)
            squares_w(BLOCKS - 1)
            deviation_w(BLOCKS - 1)
            relu1(2)
            relu1(BLOCKS - 1)
            relu2(2)
            relu2(BLOCKS - 1)

        @block.vector
        def _(dve):
            def recip_a(u, m):
                dve.wait_ge(A_sd, u + 1)
                dve.reciprocal(rA[0:ROWS, m % 2, :], sdA[0:ROWS, m % 2, :]).then_inc(A_recip, 1)

            def norm_a(u, m):
                dve.wait_ge(A_recip, u + 1)
                if u >= 2:
                    dve.wait_ge(B_done, u - 1)
                for g in range(UG):
                    last = dve.scalar_tensor_tensor(
                        out=y1[0:ROWS, m % 2, g, :], in0=psA[m % 2][0:ROWS, g * E:(g + 1) * E],
                        scalar=rA[0:ROWS, m % 2, g:g + 1], in1=gs_b[0:ROWS, :], op0=ALU.mult, op1=ALU.mult)
                last.then_inc(y1_ready, 1)

            def sums_b(u, m):
                dve.wait_ge(B_squared, u + 1)
                dve.tensor_reduce(ssB[:, m % 2, :], sqB[:, m % 2, :].rearrange("p (s j) -> p s j", j=PROJ),
                                  AX, ALU.add).then_inc(B_summed, 1)

            def recip_b(u, m):
                dve.wait_ge(B_sd, u + 1)
                dve.reciprocal(rB[:, m % 2, :], sdB[:, m % 2, :]).then_inc(B_recip, 1)

            def norm_b(u, m):
                dve.wait_ge(B_recip, u + 1)
                if u >= 2:
                    dve.wait_ge(Z_done, u - 1)
                dve.tensor_tensor(T[:, m % 2, :, 1:], psB[m % 2][:, :].rearrange("p (s j) -> p s j", j=PROJ),
                                  rB[:, m % 2, :].rearrange("p (s o) -> p s o", o=1).broadcast_to([P, US, PROJ]),
                                  ALU.mult).then_inc(T_normed, 1)

            def scale_b(u, m):
                dve.wait_ge(T_normed, u + 1)
                dve.tensor_tensor(T[:, m % 2, :, 1:], T[:, m % 2, :, 1:],
                                  gsi_b.rearrange("p (o j) -> p o j", o=1).broadcast_to([P, US, PROJ]),
                                  ALU.mult).then_inc(T_scaled, 1)

            def shift_b(u, m):
                dve.wait_ge(T_scaled, u + 1)
                dve.tensor_tensor(T[:, m % 2, :, 1:], T[:, m % 2, :, 1:],
                                  bsi_b.rearrange("p (o j) -> p o j", o=1).broadcast_to([P, US, PROJ]),
                                  ALU.add).then_inc(T_dve, 1)

            def recip_w(b):
                dve.wait_ge(W_sd, b + 1)
                dve.reciprocal(rO[:, :], sdO[:, :]).then_inc(W_recip, 1)

            def norm_w(b):
                dve.wait_ge(W_recip, b + 1)
                if b >= 1:
                    dve.wait_ge(z_ready, b)
                dve.tensor_tensor(zn[:, :, :], psW[b % 2][:, 0:KZ * BS].rearrange("p (k s) -> p k s", k=KZ),
                                  rO[:, :].rearrange("p (o s) -> p o s", o=1).broadcast_to([P, KZ, BS]),
                                  ALU.mult).then_inc(W_normed, 1)

            def scale_z(b):
                dve.wait_ge(W_normed, b + 1)
                for k in range(KZ):
                    last = dve.tensor_scalar(zT[:, k, b * BS:(b + 1) * BS], zn[:, k, :], gl_c[:, k:k + 1],
                                             bl_c[:, k:k + 1], ALU.mult, ALU.add)
                last.then_inc(z_ready, 1)

            dve.memset(eps_c[:, :], EPS).then_inc(prep, 1)
            dve.memset(ones[:, :], 1.0).then_inc(prep, 1)
            dve.wait_ge(d_small, 16)
            dve.tensor_reduce(means[0:ROWS, 0:1], wsi_sb[0:ROWS, :], AX, ALU.add).then_inc(prep, 1)
            dve.tensor_reduce(means[:, 1:2], ws_sb, AX, ALU.add).then_inc(prep, 1)
            dve.wait_ge(prep, 4)
            dve.tensor_scalar(means[0:ROWS, 2:3], means[0:ROWS, 0:1], -1.0 / PROJ, None, ALU.mult)
            dve.tensor_scalar(means[:, 3:4], means[:, 1:2], -1.0 / E, None, ALU.mult).then_inc(prep, 1)
            dve.wait_ge(prep, 5)
            dve.scalar_tensor_tensor(out=wsi_0[:, :], in0=wsim_sb[0:ROWS, :], scalar=means[0:ROWS, 2:3],
                                     in1=wsi_sb[0:ROWS, :], op0=ALU.mult, op1=ALU.add).then_inc(prep, 1)
            dve.scalar_tensor_tensor(out=ws_c[:, :], in0=wsm_sb, scalar=means[:, 3:4],
                                     in1=ws_sb, op0=ALU.mult, op1=ALU.add).then_inc(prep, 1)
            dve.wait_ge(wsi_summed, 1)
            dve.tensor_copy(wsi_c[:, :], psZ[0:ROWS + 1, 0:GS * PROJ]).then_inc(prep, 1)
            dve.wait_ge(x_mul, 1)
            for s in range(4):
                last = dve.bn_stats(xstat[:, s, :], psX[:, s * E:(s + 1) * E])
            last.then_inc(prep, 1)
            dve.wait_ge(prep, X_STAT)
            for s in range(4):
                last = dve.bn_aggr(xmv[:, s, :], xstat[:, s, :])
            last.then_inc(prep, 1)
            dve.wait_ge(d_rows, 16)

            def norm_x():
                dve.wait_ge(x_sd, 1)
                dve.reciprocal(xr[:, :], xsd[:, :]).then_inc(prep, 1)
                dve.wait_ge(prep, X_R)
                for s in range(4):
                    last = dve.tensor_scalar(xn[:, s, :], psX[:, s * E:(s + 1) * E], xmv[:, s, 0:1], xr[:, s:s + 1],
                                             ALU.subtract, ALU.mult)
                last.then_inc(prep, 1)

            def scale_x():
                dve.wait_ge(prep, X_N)
                dve.tensor_tensor(xg[:, :, :], xn[:, :, :],
                                  gd_b.rearrange("p (o e) -> p o e", o=1).broadcast_to([P, 4, E]),
                                  ALU.mult).then_inc(prep, 1)
                dve.wait_ge(prep, X_G)
                dve.tensor_tensor(xb[:, :, :], xg[:, :, :],
                                  bd_b.rearrange("p (o e) -> p o e", o=1).broadcast_to([P, 4, E]),
                                  ALU.add).then_inc(x_tr, 1)

            def center_wl(j):
                dve.wait_ge(wl_summed, j + 1)
                last = dve.tensor_scalar(wl_sb[:, j, :], wl_sb[:, j, :], wl_mean[:, j:j + 1], None, ALU.add)
                if j == JQ - 1:
                    last.then_inc(wl_ready, 1)

            def step(t):
                if 0 <= t - 2 < UNITS:
                    norm_b(t - 2, (t - 2) % BU)
                if 0 <= t < UNITS:
                    norm_a(t, t % BU)
                if t == 0:
                    norm_x()
                b, n = (t - FIRST_W) // BU, (t - FIRST_W) % BU
                if b in (1, 2) and n == 3:
                    norm_w(b - 1)
                if 0 <= t - 2 < UNITS and not on_pool(t - 2):
                    scale_b(t - 2, (t - 2) % BU)
                if 0 <= t - 1 < UNITS:
                    sums_b(t - 1, (t - 1) % BU)
                if t == 1:
                    scale_x()
                if 0 <= t - 2 < UNITS and on_pool(t - 2):
                    scale_b(t - 2, (t - 2) % BU)
                if b in (1, 2) and n == 2:
                    recip_w(b - 1)
                if 0 <= t - 2 < UNITS and not on_pool(t - 2):
                    shift_b(t - 2, (t - 2) % BU)
                if 0 <= t - 1 < UNITS:
                    recip_b(t - 1, (t - 1) % BU)
                if t + 1 < UNITS:
                    recip_a(t + 1, (t + 1) % BU)
                if 3 <= t < 3 + JQ:
                    center_wl(t - 3)

            def copy_y(b):
                dve.wait_ge(y_done, b + 1)
                dve.tensor_copy(y_sb[:, b * BS:(b + 1) * BS],
                                psH[b][0:1, K2 * BS:(K2 + 1) * BS]).then_inc(y_copied, 1)

            recip_a(0, 0)
            for t in range(0, UNITS + 1):
                step(t)
                if t == 26:
                    copy_y(0)
            step(UNITS + 1)
            recip_w(2)
            norm_w(2)
            copy_y(1)
            recip_w(BLOCKS - 1)
            norm_w(BLOCKS - 1)
            scale_z(BLOCKS - 1)
            copy_y(2)
            copy_y(BLOCKS - 1)


def kernel(**inputs):
    import numpy as np
    import concourse.bacc as bacc
    from concourse.bass_utils import run_bass_kernel_spmd

    x = {k: np.asarray(v) for k, v in inputs.items()}
    tables = [x[f"tbl_{n}"] for n in range(NSP)]

    def chunks(a):
        return np.ascontiguousarray(a.reshape(-1, 2, ROWS).transpose(1, 0, 2).reshape(2, PAIRS, P)
                                    .transpose(2, 1, 0).reshape(P, 2 * PAIRS))

    def on_partitions(a):
        return np.ascontiguousarray(a.reshape(-1, P, a.shape[1]).transpose(1, 0, 2))

    def diagonal(a, n):
        d = np.zeros((n, a.shape[0], n, a.shape[1]), a.dtype)
        for i in range(n):
            d[i, :, i, :] = a
        return d.reshape(n * a.shape[0], n * a.shape[1])

    starts = np.cumsum([0] + [t.shape[0] for t in tables[:-1]]).astype(np.int32)
    gather_ones = np.eye(ROWS, ROWS + 1, dtype=np.float32)
    gather_ones[:, ROWS] = 1.0
    q, i, j = np.meshgrid(np.arange(4), np.arange(1, PROJ + 1), np.arange(JQ), indexing="ij")
    j = q * JQ + j
    pairs = PROJ * (PROJ + 1) // 2
    at = np.where(i > j, i * (i - 1) // 2 + j, pairs).reshape(P, JQ)
    wl = x["L0_rec_Wl"].T
    wl = np.concatenate([wl, np.zeros((1, FLIN), wl.dtype)])[at]
    w1 = x["W_top1"]
    cols = np.concatenate([x["b_top1"].reshape(K1, P), x["b_top2"].reshape(K2, P), x["W_top3"].reshape(K2, P),
                           x["L0_rec_gl"][:FOUT].reshape(KZ, P), x["L0_rec_bl"][:FOUT].reshape(KZ, P)]).T

    def full(a):
        return np.concatenate([a, np.zeros((P - a.shape[0], a.shape[1]), a.dtype)])

    arrays = {
        "table": np.concatenate(tables, axis=0),
        "ids": np.stack([chunks(x["ids"]), chunks(np.broadcast_to(starts, (BATCH, NSP)))], axis=1),
        "small": np.concatenate([full(a) for a in (
            on_partitions(x["L0_rec_Wd"].T).reshape(P, KD * E),
            diagonal(x["L0_rec_Ws"].T, 2), diagonal(np.ones((DSP, E), np.float32), 2),
            diagonal(x["L0_rec_Wsi"].T, GS), diagonal(np.ones((NSP, PROJ), np.float32), GS),
            gather_ones, np.eye(P, dtype=np.float32), cols)], axis=1),
        "rows": np.concatenate([x[f"L0_rec_{n}"] for n in ("gs", "gd", "bd", "gsi", "bsi")])[None, :],
        "bs_rows": np.ascontiguousarray(np.broadcast_to(x["L0_rec_bs"], (1, 2, UG, E))),
        "dense": on_partitions(x["r_dense_t"].T),
        "wl": wl,
        "w1": on_partitions(np.concatenate([w1[:FOUT], w1[FLIN:]])),
        "w2": on_partitions(x["W_top2"]),
    }
    nc = bacc.Bacc("TRN2", target_bir_lowering=False, num_devices=1)
    args = [nc.dram_tensor(f"in_{n}", a.shape, mybir.dt.from_np(a.dtype), kind="ExternalInput").ap()
            for n, a in arrays.items()]
    out = nc.dram_tensor("out_y", (BATCH, 1), F32, kind="ExternalOutput").ap()
    tower(nc, *args, out)
    r = run_bass_kernel_spmd(nc, [{f"in_{n}": a for n, a in arrays.items()}], core_ids=[0])
    return r.results[0]["out_y"]
```
